# Optimizing a Trainium2 kernel written in Bass

```python
import numpy as np
import jax
import jax.numpy as jnp

def _softmax(x, axis=-1):
    return jax.nn.softmax(x, axis=axis)

def _gelu(x):
    return jax.nn.gelu(x, approximate=True)

def _silu(x):
    return jax.nn.silu(x)

def _sigmoid(x):
    return jax.nn.sigmoid(x)

def _layernorm(x, axis=-1, eps=1e-05):
    m = jnp.mean(x, axis=axis, keepdims=True)
    v = jnp.var(x, axis=axis, keepdims=True)
    return (x - m) / jnp.sqrt(v + eps)

def _scatter_add(tgt, idx, src, axis=0):
    return tgt.at[idx].add(src)

def _segment_sum(src, seg, n):
    return jax.ops.segment_sum(src, seg, n)
kernel_name = 'mk_conv_preact_d2_conv_nhwc256_r4_504b0c'

def setup_inputs(seed: int=0):
    np.random.seed(seed)
    _w = jnp.asarray

    def _rec_inputs():
        import jax
        import jax.numpy as jnp
        _gk = jax.random.key(seed)
        x = 7.22e-05 + 1 * jax.random.normal(jax.random.fold_in(_gk, 1), (32, 32, 32, 64), jnp.float32)
        return x
    x = _rec_inputs()

    def _L0_conv_setup():
        import jax, jax.numpy as jnp
        import numpy as np
        K = 4
        STEPS = 3
        TOP_N = 2
        HEADS = 2
        DIM_HEAD = 16
        ROUTE_TEMP = 1.5
        C = 64

        def conv3x3(x, w, b):
            y = jax.lax.conv_general_dilated(x, w, window_strides=(1, 1), padding='SAME', dimension_numbers=('NHWC', 'HWIO', 'NHWC'))
            return y + b
        key = jax.random.key(seed)
        ks = jax.random.split(key, 8)
        B, H, W = (32, 32, 32)
        D = HEADS * DIM_HEAD
        glorot = jax.nn.initializers.glorot_uniform()
        x = jax.random.normal(ks[0], (B, H, W, C), dtype=jnp.float32)
        q = glorot(ks[1], (HEADS, DIM_HEAD), jnp.float32)
        Wk = glorot(ks[2], (C, D), jnp.float32)
        Wv = glorot(ks[3], (C, D), jnp.float32)
        Wmlp = glorot(ks[4], (D, K), jnp.float32)
        alpha = jnp.zeros((), jnp.float32)
        We = glorot(ks[5], (K * 3, 3, C, C), jnp.float32).reshape(K, 3, 3, C, C)
        be = jnp.zeros((K, C), jnp.float32)
        return {'x': x, 'q': q, 'Wk': Wk, 'Wv': Wv, 'Wmlp': Wmlp, 'alpha': alpha, 'We': We, 'be': be}
    _L0_conv_all = _L0_conv_setup()
    _L0_conv_in = {k: v for k, v in _L0_conv_all.items() if k in ('q', 'Wk', 'Wv', 'Wmlp', 'alpha', 'We', 'be')}
    del _L0_conv_all

    def _L1_conv_setup():
        import jax, jax.numpy as jnp
        import numpy as np
        F = 64
        K = 3
        G = 16
        RR = 4
        BN_EPS = 0.001
        key = jax.random.key(seed)
        ks = jax.random.split(key, 8)
        C = 64
        Cr = F // RR
        KKG = K * K * G
        s = lambda k, sh, fan: jax.random.normal(k, sh, jnp.float32) * (1.0 / np.sqrt(fan))
        return {'x': jax.random.normal(ks[0], (4, 32, 32, C), jnp.float32), 'Wr': s(ks[1], (C, Cr), C), 'br': jnp.zeros((Cr,), jnp.float32), 'gamma': jnp.ones((Cr,), jnp.float32), 'beta': jnp.zeros((Cr,), jnp.float32), 'mean': jax.random.normal(ks[2], (Cr,), jnp.float32) * 0.1, 'var': jax.random.uniform(ks[3], (Cr,), jnp.float32, 0.5, 1.5), 'Ws': s(ks[4], (Cr, KKG), Cr), 'bs': jnp.zeros((KKG,), jnp.float32), 'Wi': s(ks[5], (C, F), C), 'bi': jnp.zeros((F,), jnp.float32)}
    _L1_conv_all = _L1_conv_setup()
    _L1_conv_in = {k: v for k, v in _L1_conv_all.items() if k in ('Wr', 'br', 'gamma', 'beta', 'mean', 'var', 'Ws', 'bs', 'Wi', 'bi')}
    del _L1_conv_all
    return {'x': x, 'L0_conv_q': _L0_conv_in['q'], 'L0_conv_Wk': _L0_conv_in['Wk'], 'L0_conv_Wv': _L0_conv_in['Wv'], 'L0_conv_Wmlp': _L0_conv_in['Wmlp'], 'L0_conv_alpha': _L0_conv_in['alpha'], 'L0_conv_We': _L0_conv_in['We'], 'L0_conv_be': _L0_conv_in['be'], 'L1_conv_Wr': _L1_conv_in['Wr'], 'L1_conv_br': _L1_conv_in['br'], 'L1_conv_gamma': _L1_conv_in['gamma'], 'L1_conv_beta': _L1_conv_in['beta'], 'L1_conv_mean': _L1_conv_in['mean'], 'L1_conv_var': _L1_conv_in['var'], 'L1_conv_Ws': _L1_conv_in['Ws'], 'L1_conv_bs': _L1_conv_in['bs'], 'L1_conv_Wi': _L1_conv_in['Wi'], 'L1_conv_bi': _L1_conv_in['bi']}

def reference(x, L0_conv_q, L0_conv_Wk, L0_conv_Wv, L0_conv_Wmlp, L0_conv_alpha, L0_conv_We, L0_conv_be, L1_conv_Wr, L1_conv_br, L1_conv_gamma, L1_conv_beta, L1_conv_mean, L1_conv_var, L1_conv_Ws, L1_conv_bs, L1_conv_Wi, L1_conv_bi):
    import jax
    import jax.numpy as jnp

    def _L0_conv_ref(x, q, Wk, Wv, Wmlp, alpha, We, be):
        import jax, jax.numpy as jnp
        import numpy as np
        K = 4
        STEPS = 3
        TOP_N = 2
        HEADS = 2
        DIM_HEAD = 16
        ROUTE_TEMP = 1.5
        C = 64

        def conv3x3(x, w, b):
            y = jax.lax.conv_general_dilated(x, w, window_strides=(1, 1), padding='SAME', dimension_numbers=('NHWC', 'HWIO', 'NHWC'))
            return y + b
        B, H, W, Cc = x.shape
        S = H * W
        allowed = jnp.ones((B, K), x.dtype)
        last_oh = jax.nn.one_hot(jnp.full((B,), K - 1), K, dtype=x.dtype)
        scale = jnp.asarray(S, x.dtype)
        a = jax.nn.softplus(alpha)
        for t in range(STEPS):
            k = jnp.einsum('bhwc,cd->bhwd', x, Wk).reshape(B, S, HEADS, DIM_HEAD)
            v = jnp.einsum('bhwc,cd->bhwd', x, Wv).reshape(B, S, HEADS, DIM_HEAD)
            attn = jax.nn.softmax(jnp.einsum('nd,bsnd->bns', q, k) / jnp.sqrt(jnp.asarray(DIM_HEAD, x.dtype)), axis=-1)
            pooled = jnp.einsum('bns,bsnd->bnd', attn, v).reshape(B, HEADS * DIM_HEAD)
            logits = pooled @ Wmlp
            attn_map = attn.mean(axis=1).reshape(B, H, W, 1)
            masked_logits = jnp.where(allowed > 0.5, logits, jnp.asarray(-1000000000.0, x.dtype))
            weights = jax.nn.softmax(masked_logits / ROUTE_TEMP, axis=-1)
            top_vals, top_idx = jax.lax.top_k(weights, TOP_N)
            mask_oh = jax.nn.one_hot(top_idx, K, dtype=x.dtype).sum(axis=1)
            wm = weights * mask_oh
            wsel = wm / (wm.sum(axis=-1, keepdims=True) + 1e-09)
            x_mod = x * (1.0 + attn_map * scale * a)
            y = jnp.zeros_like(x)
            for e in range(K):
                ye = conv3x3(x_mod, We[e], be[e])
                y = y + wsel[:, e][:, None, None, None] * ye
            top1 = top_idx[:, 0]
            not_last = (top1 != K - 1).astype(x.dtype)
            delta = jax.nn.one_hot(top1, K, dtype=x.dtype) * not_last[:, None]
            allowed = jnp.clip(allowed - delta, 0.0, 1.0)
            allowed = jnp.maximum(allowed, last_oh)
            x = y
        return x

    def _L1_conv_ref(x, Wr, br, gamma, beta, mean, var, Ws, bs, Wi, bi):
        import jax, jax.numpy as jnp
        import numpy as np
        F = 64
        K = 3
        G = 16
        RR = 4
        BN_EPS = 0.001
        B, H, W, _ = x.shape
        KK = K * K
        r = jnp.einsum('bhwc,cd->bhwd', x, Wr) + br
        r = jax.nn.relu((r - mean) * jax.lax.rsqrt(var + BN_EPS) * gamma + beta)
        w = jnp.einsum('bhwd,dk->bhwk', r, Ws) + bs
        w = w.reshape(B, H, W, G, KK)[:, :, :, :, None, :]
        xi = jnp.einsum('bhwc,cf->bhwf', x, Wi) + bi
        pad = (K - 1) // 2
        xp = jnp.pad(xi, ((0, 0), (pad, pad), (pad, pad), (0, 0)))
        patches = jnp.stack([xp[:, i:i + H, j:j + W, :] for i in range(K) for j in range(K)], axis=3)
        patches = patches.reshape(B, H, W, G, F // G, KK)
        out = jnp.sum(w * patches, axis=-1)
        return out.reshape(B, H, W, F)

    def _gn(v, G=32, eps=1e-05):
        B_, H_, W_, C_ = v.shape
        g = v.reshape(B_, H_, W_, G, C_ // G)
        m = jnp.mean(g, axis=(1, 2, 4), keepdims=True)
        s = jnp.var(g, axis=(1, 2, 4), keepdims=True)
        return ((g - m) / jnp.sqrt(s + eps)).reshape(v.shape)

    def _ln_c(v, eps=1e-06):
        m = jnp.mean(v, axis=-1, keepdims=True)
        s = jnp.var(v, axis=-1, keepdims=True)
        return (v - m) / jnp.sqrt(s + eps)

    def _ln_t(v, eps=1e-05):
        m = jnp.mean(v, axis=-1, keepdims=True)
        s = jnp.var(v, axis=-1, keepdims=True)
        return (v - m) / jnp.sqrt(s + eps)

    def _to_tokens(v):
        B_, H_, W_, C_ = v.shape
        return v.reshape(B_, H_ * W_, C_)

    def _from_tokens(t, like):
        return t.reshape(like.shape)
    x = x + _L0_conv_ref(_gn(x), L0_conv_q, L0_conv_Wk, L0_conv_Wv, L0_conv_Wmlp, L0_conv_alpha, L0_conv_We, L0_conv_be)
    x = x + _L1_conv_ref(_gn(x), L1_conv_Wr, L1_conv_br, L1_conv_gamma, L1_conv_beta, L1_conv_mean, L1_conv_var, L1_conv_Ws, L1_conv_bs, L1_conv_Wi, L1_conv_bi)
    return x

_drawn_inputs = setup_inputs


def setup_inputs(seed=0):
    import zlib

    import numpy as np

    out = dict(_drawn_inputs(seed))
    spreads = {'L0_conv_be': (0.0, 0.1),
     'L1_conv_br': (0.0, 0.1),
     'L1_conv_gamma': (1.0, 0.2),
     'L1_conv_beta': (0.0, 0.1),
     'L1_conv_bs': (0.0, 0.1),
     'L1_conv_bi': (0.0, 0.1)}
    factors = {}
    for name, (base, spread) in spreads.items():
        noise = np.random.default_rng([zlib.crc32(name.encode()), seed]).standard_normal(out[name].shape)
        drawn = base * np.exp(spread * noise) if base else spread * noise
        out[name] = jnp.asarray(drawn.astype(out[name].dtype))
    for name, factor in factors.items():
        out[name] = (out[name] * factor).astype(out[name].dtype)
    return out
```

```python
from contextlib import ExitStack

import numpy as np

import concourse.bass as bass
from concourse import mybir

F32 = mybir.dt.float32
F32R = mybir.dt.float32r
BF16 = mybir.dt.bfloat16
ALU = mybir.AluOpType
ACT = mybir.ActivationFunctionType
AX = mybir.AxisListType

B, H, W, C = 32, 32, 32, 64
S = H * W
NP = B // 2
GP = NP // 2
HW = S // 2
PW = W + 2
PS = PW * PW
K = 4
HEADS, DH = 2, 16
D = HEADS * DH
STEPS = 3
PHASES = 2 * STEPS
TEMP = 1.5
TAPS = 9
CR = 16
G16 = 16
GN_EPS = 1e-5
BN_EPS = 1e-3
PARTS = 3
AR = PARTS * 4 * GP
RR = 98
T = S // 128

PROLOGUE_USES = (
    [("turn", k) for k in range(GP)] + [("gn", 0)] + [("scores",)]
    + [("spread", i, n) for i in range(GP) for n in range(HEADS)] + [("logits",)]
    + [("turn", k) for k in range(GP, NP)] + [("gn", 1)] + [("map", 0)]
)


def slot_uses(j):
    uses = [(("map", (j + 1) % GP), 0)]
    if j == 0:
        uses += [(("scores",), 6)]
    if 2 <= j <= 5:
        uses += [(("spread", 2 * (j - 2) + m // 2, m % 2), 1 + 2 * m) for m in range(4)]
    if j == 6:
        uses += [(("logits",), 4)]
    return uses


PHASE_USES = [key for j in range(GP) for key, _ in slot_uses(j)]
LAST_USES = [("map", i) for i in range(1, GP)]
assert len(PHASE_USES) % 2 == 0


class Use:

    def __init__(self, p, key):
        if isinstance(p, int) and p == -1:
            at = PROLOGUE_USES.index(key)
            self.unit, self.before, self.full = at % 2, at // 2, at + 1
        elif isinstance(p, int) and p == PHASES - 1:
            at = len(PROLOGUE_USES) + p * len(PHASE_USES) + LAST_USES.index(key)
            self.unit, self.before, self.full = at % 2, at // 2, at + 1
        else:
            at = len(PROLOGUE_USES) + PHASE_USES.index(key)
            self.unit = at % 2
            self.before = p * (len(PHASE_USES) // 2) + at // 2
            self.full = p * len(PHASE_USES) + at + 1
        self.freed = self.before + 1


class Steps:

    def __init__(self, eng, sem):
        self.eng, self.sem, self.base, self.n = eng, sem, 0, 0

    def start(self, base):
        self.base, self.n = base, 0

    def then(self, instruction):
        self.n += 1
        instruction.then_inc(self.sem, 1)
        self.eng.wait_ge(self.sem, self.base + self.n)


SOFT_STEPS, ROUTE_STEPS = 7, 23
POW_STEP = 4
DIRECT = 4
LO_DVE = (1, 7)
LO_POOL = tuple(t for t in range(TAPS) if t != DIRECT and t not in LO_DVE)
SPLIT = tuple(t for t in range(TAPS) if t != DIRECT)
RING = 3
LAG = 3


def build(nc, A, out):
    ctx = ExitStack()
    with ctx:
        def sb(name, shape, dt=F32):
            return ctx.enter_context(nc.sbuf_tensor(name, shape, dt))

        def sem(name):
            return ctx.enter_context(nc.semaphore(name))

        xin = sb("xin", [128, NP, S])
        x = sb("x", [128, NP, S])
        with ExitStack() as routed_only:
            experts = routed_only.enter_context(nc.sbuf_tensor("experts", [128, K, TAPS * C], F32))
        sum_sel = sb("sum_sel", [128, TAPS, 128], F32R)
        wse = sb("wse", [RR, TAPS, 128], F32R)
        comb = sb("comb", [128, TAPS, C])
        whi = sb("whi", [128, 2, TAPS, 128], F32R)
        wlo = sb("wlo", [128, 2, TAPS, 128], F32R)
        xhi = sb("xhi", [128, 2, PW, PW], F32R)
        xlo = sb("xlo", [128, 2, PW, PW], F32R)
        xm = sb("xm", [128, S])
        work = sb("work", [128, S])
        attn = work[0:AR, :]
        parts = sb("parts", [AR, 2, S], BF16)
        spread_sel = sb("spread_sel", [AR, GP * 3, 128], BF16)
        ident = sb("ident", [128, 128])
        pair_avg = sb("pair_avg", [128, 128])
        same_image = sb("same_image", [128, 128])
        wi = sb("wi", [128, 128])
        wr = sb("wr", [128, AR])
        wq8 = sb("wq8", [128, 800])
        wk_s = sb("wk_s", [128, D])
        q_s = sb("q_s", [128, D])
        wv_s = sb("wv_s", [128, D])
        wm_s = sb("wm_s", [128, D * K])
        tmp32 = sb("tmp32", [128, HEADS, K, DH])
        wq = sb("wq", [128, HEADS])
        gate = sb("gate", [128, HEADS, K])
        be_s = sb("be_s", [128, K])
        earlier = sb("earlier", [128, K, K])
        alpha = sb("alpha", [128, 1])
        sp = sb("sp", [128, 4])
        gain = sb("gain", [128, 1])
        one = sb("one", [128, 1])
        mhalf = sb("mhalf", [128, 2 * NP])
        masks = sb("masks", [RR, 4])
        rpar = sb("rpar", [AR, 5])
        rsc = sb("rsc", [AR, 4])
        bi_s = sb("bi_s", [128, 1])
        stats = sb("stats", [128, NP, 2, 6])
        mv = sb("mv", [128, NP, 2])
        gnt = sb("gnt", [128, 5, NP])
        rstd = sb("rstd", [128, NP])
        nmr = sb("nmr", [128, NP])
        soft = sb("soft", [AR, 4])
        pooled = sb("pooled", [128, GP, HEADS])
        zt = sb("zt", [128, 2, GP, K])
        rt = sb("rt", [128, 12, GP, K])
        rs = sb("rs", [128, 6, GP])
        cmp = sb("cmp", [128, 3, GP, K, K])
        wsel = sb("wsel", [128, GP, K])
        allowed = sb("allowed", [128, 2, GP, K])
        bias = sb("bias", [128, NP])

        stage = x[:, GP:NP, :].rearrange("p a b -> p (a b)")
        st_sel = stage[0:AR, 0:3 * GP * 128]
        st_sum = stage[:, 4096:4096 + TAPS * 128]
        st_ws = stage[0:RR, 5248:5248 + TAPS * G16]
        st_exp = stage[0:RR, 5392:5392 + TAPS * C]
        st_bd = stage[0:RR, 5968:5968 + TAPS * 128].rearrange("p (t c) -> p t c", t=TAPS)
        xpix = [x[:, NP - 2 + n, :].rearrange("p (t c) -> p t c", t=T) for n in range(2)]

        conv = ctx.enter_context(nc.psum_tensor("conv", [128, 2, S], F32))
        att = ctx.enter_context(nc.psum_tensor("att", [128, 2, S], F32))

        consts_in = sem("consts_in")
        late_consts_in = sem("late_consts_in")
        late_setup = sem("late_setup")
        wse_ready = sem("wse_ready")
        pix_in = [sem("pix_in0"), sem("pix_in1")]
        zeroed = sem("zeroed")
        setup = sem("setup")
        setup_pool = sem("setup_pool")
        setup_act = sem("setup_act")
        setup_done = sem("setup_done")
        att_full = sem("att_full")
        att_free = [sem("att_free0"), sem("att_free1")]
        mv_ready = sem("mv_ready")
        gn_step = sem("gn_step")
        rstd_ready = sem("rstd_ready")
        nmr_ready = sem("nmr_ready")
        x_ready = sem("x_ready")
        soft_step = sem("soft_step")
        negmax_ready = sem("negmax_ready")
        exp_ready = sem("exp_ready")
        parts_ready = sem("parts_ready")
        gated_ready = sem("gated_ready")
        route_step = sem("route_step")
        shifted_ready = sem("shifted_ready")
        rexp_ready = sem("rexp_ready")
        bias_ready = sem("bias_ready")
        xm_ready = sem("xm_ready")
        xhi_ready = sem("xhi_ready")
        xlo_ready = sem("xlo_ready")
        comb_step = sem("comb_step")
        whi_ready = sem("whi_ready")
        wlo_ready = sem("wlo_ready")
        conv_full = sem("conv_full")
        x1_step = sem("x1_step")
        mv2_ready = sem("mv2_ready")
        gn2_full = sem("gn2_full")
        pads_zeroed = sem("pads_zeroed")
        misc_full = sem("misc_full")
        misc_free = sem("misc_free")
        xn_ready = sem("xn_ready")
        xi_ready = sem("xi_ready")
        r_ready = sem("r_ready")
        rhi_ready = sem("rhi_ready")
        rstk_ready = sem("rstk_ready")
        exp_full = sem("exp_full")
        prod_ready = sem("prod_ready")
        hi_ready = sem("hi_ready")
        lo_dve_ready = sem("lo_dve_ready")
        lo_pool_ready = sem("lo_pool_ready")
        sum_done = sem("sum_done")
        fin_ready = sem("fin_ready")
        stored = [sem("stored0"), sem("stored1")]

        flat = x[:, :, :].rearrange("p a b -> p (a b)")
        prod = [flat[:, n * S:(n + 1) * S] for n in range(RING)]
        xn = [flat[:, (3 + n) * S:(4 + n) * S] for n in range(2)]
        r96 = flat[0:AR, 5 * S:6 * S]
        fin = flat[:, 6 * S:7 * S]
        pix = [flat[:, (7 + n) * S:(8 + n) * S].rearrange("p (t c) -> p t c", t=T) for n in range(2)]
        xip = [flat[:, 9 * S + n * PS:9 * S + (n + 1) * PS].rearrange("p (a b) -> p a b", a=PW)
               for n in range(2)]

        def pad_flat(t, n):
            return t[:, n, :, :].rearrange("p a b -> p (a b)")[:, 0:S]

        hi = [pad_flat(xhi, 0), pad_flat(xhi, 1), pad_flat(whi, 0)]
        lo = [pad_flat(xlo, 0), pad_flat(xlo, 1), pad_flat(wlo, 0)]
        rstk = [pad_flat(whi, 1), pad_flat(wlo, 1)]

        def img(ap):
            return ap.rearrange("p (a b) -> p a b", a=H)

        def inner(padded, n):
            return padded[:, n, 1:H + 1, 1:W + 1]

        def halves():
            return ((h, slice(h * HW, (h + 1) * HW)) for h in range(2))

        CONSTS = [
            (st_sel, A["c_spread"]), (ident[:, :], A["c_ident"]), (pair_avg[:, :], A["c_pair"]),
            (same_image[:, :], A["c_same"]), (masks[:, :], A["c_masks"]),
            (earlier[:, :, :].rearrange("p a b -> p (a b)"), A["c_earlier"].partition_broadcast(128)),
            (q_s[:, :], A["q"].partition_broadcast(128)),
            (wm_s[:, :], A["Wmlp"].partition_broadcast(128)),
            (alpha[:, :], A["alpha"].partition_broadcast(128)),
            (rpar[:, :], A["rpar"]),
        ]
        for n in range(2):
            p = slice(64 * n, 64 * n + 64)
            CONSTS += [
                (wk_s[p, :], A["Wk"]), (wv_s[p, :], A["Wv"]), (be_s[p, :], A["be"]),
                (experts[p, :, :].rearrange("p k (t c) -> p (k t) c", t=TAPS), A["We"].rearrange("t i o -> i t o")),
                (bi_s[p, :], A["bi"]),
            ]
        LATE_CONSTS = [(st_sum, A["c_sum"]), (st_ws[AR:RR, :], A["bs"].partition_broadcast(2))]
        LATE_CONSTS += [(st_ws[CR * a:CR * a + CR, :], A["Ws"]) for a in range(2 * PARTS)]
        BLOCKS = [(wi[64 * n:64 * n + 64, 64 * n:64 * n + 64], A["Wi"]) for n in range(2)]
        BLOCKS += [(wr[64 * n:64 * n + 64, 32 * a + CR * n:32 * a + CR * n + CR], A["Wr"])
                   for n in range(2) for a in range(PARTS)]
        CONSTS_IN = 16 * (len(CONSTS) + len(BLOCKS))
        ZEROS = 7

        block = ctx.enter_context(nc.Block())

        @block.sync
        def _(eng):
            def load_pair(k, n):
                for m in range(2):
                    eng.dma_start(xpix[n][:, :, 64 * m:64 * m + 64],
                                  A["x"][2 * k + m, :, :].rearrange("(p t) c -> p t c", t=T)).then_inc(pix_in[n], 16)

            load_pair(0, 0)
            load_pair(1, 1)
            for dst, src in CONSTS:
                eng.dma_start(dst, src).then_inc(consts_in, 16)
            eng.wait_ge(zeroed, ZEROS)
            for dst, src in BLOCKS:
                eng.dma_start(dst, src).then_inc(consts_in, 16)
            with eng.Fori(1, GP // 2 + 1) as i:
                for n in range(2):
                    eng.wait_ge(att_free[n], i)
                    load_pair(2 * i + n, n)
            with eng.Fori(GP // 2 + 1, GP) as i:
                for n in range(2):
                    use = Use(-1, ("turn", GP + n))
                    eng.wait_ge(att_free[use.unit], i + use.freed - (GP // 2 + 1))
                    load_pair(2 * i + n, n)

            eng.wait_ge(mv2_ready, NP)
            for dst, src in LATE_CONSTS:
                eng.dma_start(dst, src).then_inc(late_consts_in, 16)

            def store_pair(k, n, uses):
                eng.wait_ge(misc_free, uses)
                for m in range(2):
                    eng.dma_start(out[2 * k + m, :, :].rearrange("(p t) c -> p t c", t=T),
                                  pix[n][:, :, 64 * m:64 * m + 64]).then_inc(stored[n], 16)

            with eng.Fori(0, GP - 1) as i:
                for n in range(2):
                    store_pair(2 * i + n, n, 6 * i + 3 * n + 7)
            for n in range(2):
                store_pair(NP - 2 + n, n, 3 * NP - 1 + n)
            for n in range(2):
                eng.wait_ge(stored[n], 2 * 16 * GP)

        @block.tensor
        def _(eng):
            def claim(use):
                if not (isinstance(use.before, int) and use.before == 0):
                    eng.wait_ge(att_free[use.unit], use.before)

            def turn(k):
                use = Use(-1, ("turn", k))
                claim(use)
                eng.wait_ge(pix_in[k % 2], 32 * (k // 2 + 1))
                for t in range(T):
                    last = nc.tensor.transpose(att[:, use.unit, 128 * t:128 * t + 128], xpix[k % 2][:, t, :], ident[:, :])
                last.then_inc(att_full, 1)

            def group_average(g):
                use = Use(-1, ("gn", g))
                claim(use)
                eng.wait_ge(mv_ready, GP * (g + 1))
                nc.tensor.matmul(att[:, use.unit, 0:2 * GP], pair_avg[:, :], mv[:, g * GP:(g + 1) * GP, :],
                                 start=True, stop=True).then_inc(att_full, 1)

            def scores(p, a, g):
                use = Use(p, ("scores",))
                claim(use)
                if isinstance(a, int) and a == 0:
                    eng.wait_ge(x_ready, GP)
                else:
                    eng.wait_ge(x_ready, NP + GP * p)
                for h, cols in halves():
                    for i in range(GP):
                        last = nc.tensor.matmul(att[0:AR, use.unit, cols], wq8[:, AR * i:AR * i + AR],
                                                x[:, g * GP + i, cols], start=(i == 0), stop=(i == GP - 1))
                last.then_inc(att_full, 1)

            def spread(p, a, g, i, n):
                use = Use(p, ("spread", i, n))
                claim(use)
                if i == 0 and n == 0:
                    eng.wait_ge(parts_ready, a + 1)
                for h, cols in halves():
                    last = nc.tensor.matmul(att[:, use.unit, cols], spread_sel[:, 3 * i + n, :], parts[:, g, cols],
                                            start=True, stop=True)
                last.then_inc(att_full, 1)

            def attention_map(p, g, i):
                use = Use(p, ("map", i))
                claim(use)
                for h, cols in halves():
                    last = nc.tensor.matmul(att[:, use.unit, cols], spread_sel[:, 3 * i + 2, :], parts[:, g, cols],
                                            start=True, stop=True)
                last.then_inc(att_full, 1)

            def logits(p, a):
                use = Use(p, ("logits",))
                claim(use)
                eng.wait_ge(gated_ready, a + 1)
                nc.tensor.matmul(att[:, use.unit, 0:GP * K], same_image[:, :],
                                 zt[:, 0, :, :], start=True, stop=True).then_inc(att_full, 1)

            def convolve(p, j, a, g, more):
                q = p * GP + j
                s = j % 2
                eng.wait_ge(xlo_ready, q + 1)
                eng.wait_ge(wlo_ready, 2 * q + 2)
                eng.wait_ge(x_ready, NP + q - 1)
                for t in range(TAPS):
                    kh, kw = divmod(t, 3)
                    for wt, xt in ((whi, xhi), (whi, xlo), (wlo, xhi)):
                        for h, cols in halves():
                            last = nc.tensor.matmul(
                                conv[:, s, cols], wt[:, s, t, :],
                                xt[:, s, kh + 16 * h:kh + 16 * h + 16, kw:kw + W],
                                start=(t == 0 and wt is whi and xt is xhi), stop=(t == TAPS - 1 and wt is wlo))
                    if t == TAPS - 1:
                        last.then_inc(conv_full, 1)
                    for key, behind in slot_uses(j):
                        if behind == t and more(key):
                            if key[0] == "map":
                                attention_map(p, a[1] if key[1] == 0 else g, key[1])
                            elif key[0] == "scores":
                                scores(p, a[0], a[1])
                            elif key[0] == "spread":
                                spread(p, a[0], a[1], key[1], key[2])
                            elif key[0] == "logits":
                                logits(p, a[0])

            eng.wait_ge(consts_in, CONSTS_IN)
            for k in range(GP):
                turn(k)
            group_average(0)
            eng.wait_ge(setup_done, 1)
            scores(-1, 0, 0)
            for i in range(GP):
                for n in range(HEADS):
                    spread(-1, 0, 0, i, n)
            logits(-1, 0)
            for k in range(GP, NP):
                turn(k)
            group_average(1)
            attention_map(-1, 0, 0)
            with eng.Fori(0, PHASES - 1) as p:
                g = eng.snap(p % 2)
                ng = eng.snap((p + 1) % 2)
                for j in range(GP):
                    convolve(p, j, (p + 1, ng), g, lambda key: True)
            for j in range(GP):
                convolve(PHASES - 1, j, None, (PHASES - 1) % 2, lambda key: key[0] == "map" and key[1] != 0)

            eng.wait_ge(mv2_ready, NP)
            nc.tensor.matmul(att[:, 1, 0:2 * NP], pair_avg[:, :], mv[:, :, :], start=True, stop=True)\
                .then_inc(gn2_full, 1)

            def project(k, s, m, weights, rows):
                if not (isinstance(m, int) and m == 0):
                    eng.wait_ge(misc_free, m)
                eng.wait_ge(xn_ready, k + 1)
                for h, cols in halves():
                    last = nc.tensor.matmul(att[0:rows, 1, cols], weights, xn[s][:, cols], start=True, stop=True)
                last.then_inc(misc_full, 1)

            def turn_back(k, m):
                eng.wait_ge(misc_free, m)
                eng.wait_ge(fin_ready, k + 1)
                cols = fin.rearrange("c (p t) -> c t p", t=T)
                for t in range(T):
                    last = nc.tensor.transpose(att[:, 1, 128 * t:128 * t + 128], cols[:, t, :], ident[:, :])
                last.then_inc(misc_full, 1)

            def expand(k, s, kk):
                e = k * TAPS + kk
                unit = (s * TAPS + kk) % 2
                if kk == 0:
                    eng.wait_ge(rstk_ready, k + 1)
                if not (isinstance(k, int) and k == 0 and kk < 2):
                    eng.wait_ge(prod_ready, e - 1)
                for h, cols in halves():
                    last = nc.tensor.matmul(conv[:, unit, cols], wse[:, kk, :], rstk[s][0:RR, cols],
                                            start=True, stop=True)
                last.then_inc(exp_full, 1)

            def add_up(k, kk):
                slot = kk % RING
                if kk == 0 and not (isinstance(k, int) and k == 0):
                    eng.wait_ge(fin_ready, k)
                if kk == DIRECT:
                    eng.wait_ge(prod_ready, k * TAPS + kk + 1)
                    passes = [(sum_sel[:, kk, :].bitcast(F32), prod[slot])]
                else:
                    if kk in LO_DVE:
                        eng.wait_ge(lo_dve_ready, k * len(LO_DVE) + LO_DVE.index(kk) + 1)
                    else:
                        eng.wait_ge(lo_pool_ready, k * len(LO_POOL) + LO_POOL.index(kk) + 1)
                    passes = [(sum_sel[:, kk, :], hi[slot]), (sum_sel[:, kk, :], lo[slot])]
                for n, (sel, src) in enumerate(passes):
                    for h, cols in halves():
                        last = nc.tensor.matmul(att[:, 0, cols], sel, src[:, cols], start=(kk == 0 and n == 0),
                                                stop=(kk == TAPS - 1 and n == len(passes) - 1))
                last.then_inc(sum_done, 1)

            def involve(k, s, first=False, last=False):
                for kk in range(TAPS):
                    expand(k, s, kk)
                    if kk >= LAG:
                        add_up(k, kk - LAG)
                    elif not first:
                        add_up(k - 1, TAPS + kk - LAG)
                    m = 2 if first else 3 * k + 1
                    if kk == 2 and not last:
                        project(k + 1, 1 - s, m, wi[:, :], 128)
                    if kk == 4 and not last:
                        project(k + 1, 1 - s, m + 1, wr[:, :], AR)
                    if kk == 6 and not first:
                        turn_back(k - 1, m if last else m + 2)

            eng.wait_ge(wse_ready, 1)
            project(0, 0, 0, wi[:, :], 128)
            project(0, 0, 1, wr[:, :], AR)
            involve(0, 0, first=True)
            with eng.Fori(0, GP - 1) as i:
                involve(2 * i + 1, 1)
                involve(2 * i + 2, 0)
            involve(NP - 1, 1, last=True)
            for kk in range(TAPS - LAG, TAPS):
                add_up(NP - 1, kk)
            turn_back(NP - 1, 3 * NP - 1)

        @block.scalar
        def _(eng):
            eng.wait_ge(setup, 2)
            nc.scalar.activation(sp[:, 1:2], sp[:, 0:1], ACT.Exp, scale=-1.0).then_inc(setup_act, 1)
            eng.wait_ge(setup_act, 1)
            nc.scalar.activation(sp[:, 2:3], sp[:, 1:2], ACT.Ln, bias=one[:, 0:1]).then_inc(setup_act, 1)

            def turned(k):
                use = Use(-1, ("turn", k))
                eng.wait_ge(att_full, use.full)
                nc.scalar.activation(xin[:, k, :].rearrange("c (p t) -> c p t", t=T),
                                     att[:, use.unit, :].rearrange("c (t p) -> c p t", t=T), ACT.Copy)\
                    .then_inc(att_free[use.unit], 1)

            def normalise(g):
                eng.wait_ge(nmr_ready, g + 1)
                for k in range(g * GP, (g + 1) * GP):
                    nc.scalar.activation(x[:, k, :], xin[:, k, :], ACT.Identity, bias=nmr[:, k:k + 1],
                                         scale=rstd[:, k:k + 1]).then_inc(x_ready, 1)

            def exponentials(p, a):
                use = Use(p, ("scores",))
                eng.wait_ge(negmax_ready, a + 1)
                nc.scalar.activation(attn, att[0:AR, use.unit, :], ACT.Exp, bias=soft[:, 1:2],
                                     accum_out=soft[:, 2:3]).then_inc(att_free[use.unit], 1)

            def route_exp(a):
                eng.wait_ge(shifted_ready, a + 1)
                nc.scalar.activation(rt[:, 3, :, :], rt[:, 2, :, :], ACT.Exp, scale=1.0 / TEMP).then_inc(rexp_ready, 1)

            def factor(p, use, q):
                eng.wait_ge(att_full, use.full)
                if not (isinstance(q, int) and q == 0):
                    eng.wait_ge(xlo_ready, q)
                nc.scalar.activation(xm[:, :], att[:, use.unit, :], ACT.Identity, bias=one[:, 0:1],
                                     scale=gain[:, 0:1]).then_inc(att_free[use.unit], 1)

            def split_hi(q, s):
                eng.wait_ge(comb_step, K * (q + 1))
                for n in range(2):
                    p = slice(64 * n, 64 * n + 64)
                    nc.scalar.activation(whi[p, s, :, 64 * n:64 * n + 64], comb[p, :, :], ACT.Copy).then_inc(whi_ready, 1)
                eng.wait_ge(xm_ready, q + 1)
                nc.scalar.activation(inner(xhi, s), img(xm[:, :]), ACT.Copy).then_inc(xhi_ready, 1)

            def empty_conv(q, s, row, a):
                eng.wait_ge(conv_full, q + 1)
                eng.wait_ge(bias_ready, a + 1)
                nc.scalar.activation(x[:, row, :], conv[:, s, :], ACT.Identity, bias=bias[:, bass.ds(row, 1)])\
                    .then_inc(x_ready, 1)

            def phase(p, g, attend):
                for j in range(GP):
                    q = p * GP + j
                    if j < GP - 1 or attend:
                        factor(p, Use(p, ("map", (j + 1) % GP)), q + 1)
                        split_hi(q + 1, (j + 1) % 2)
                    if attend and j == 0:
                        exponentials(p, p + 1)
                    if attend and j == 6:
                        route_exp(p + 1)
                    empty_conv(q, j % 2, g * GP + j, p)

            for k in range(GP):
                turned(k)
            normalise(0)
            exponentials(-1, 0)
            route_exp(0)
            for k in range(GP, NP):
                turned(k)
            normalise(1)
            eng.wait_ge(setup_done, 1)
            factor(-1, Use(-1, ("map", 0)), 0)
            split_hi(0, 0)
            with eng.Fori(0, PHASES - 1) as p:
                g = eng.snap(p % 2)
                phase(p, g, True)
            phase(PHASES - 1, (PHASES - 1) % 2, False)

            eng.wait_ge(nmr_ready, 3)
            eng.wait_ge(pads_zeroed, 4)

            def normalise2(k, s):
                nc.scalar.activation(xn[s], xin[:, k, :], ACT.Identity, bias=nmr[:, bass.ds(k, 1)],
                                     scale=rstd[:, bass.ds(k, 1)]).then_inc(xn_ready, 1)

            def empty_xi(s, m):
                eng.wait_ge(misc_full, m + 1)
                nc.scalar.activation(xip[s][:, 1:H + 1, 1:W + 1], img(att[:, 1, :]), ACT.Identity, bias=bi_s[:, 0:1])\
                    .then_inc(misc_free, 1)

            def empty_r(k, s, m):
                eng.wait_ge(misc_full, m + 1)
                if not (isinstance(k, int) and k == 0):
                    eng.wait_ge(rstk_ready, k)
                nc.scalar.activation(r96, att[0:AR, 1, :], ACT.Relu, bias=rsc[:, 3:4], scale=rsc[:, 1:2])\
                    .then_inc(misc_free, 1)
                eng.wait_ge(misc_free, m + 1)
                nc.scalar.activation(rstk[s][0:AR, :], r96, ACT.Copy).then_inc(rhi_ready, 1)

            def split_prod(k, kk, first):
                slot = kk % RING
                eng.wait_ge(prod_ready, k * TAPS + kk + 1)
                if not (first and kk < RING):
                    eng.wait_ge(sum_done, k * TAPS + kk + 1 - RING)
                nc.scalar.activation(hi[slot], prod[slot], ACT.Copy).then_inc(hi_ready, 1)

            def empty_pix(k, s, m):
                eng.wait_ge(misc_full, m + 1)
                if not (isinstance(k, int) and k < 2):
                    eng.wait_ge(stored[s], (k - s) * 16)
                nc.scalar.activation(pix[s], att[:, 1, :].rearrange("p (t c) -> p t c", t=T), ACT.Copy)\
                    .then_inc(misc_free, 1)

            def involve(k, s, first=False, last=False):
                m = 2 if first else 3 * k + 1
                if not last:
                    normalise2(k + 1, 1 - s)
                for kk in range(TAPS):
                    if kk != DIRECT:
                        split_prod(k, kk, first)
                    if kk == 3 and not last:
                        empty_xi(1 - s, m)
                    if kk == 5 and not last:
                        empty_r(k + 1, 1 - s, m + 1)
                    if kk == 7 and not first:
                        empty_pix(k - 1, 1 - s, m if last else m + 2)

            normalise2(0, 0)
            empty_xi(0, 0)
            empty_r(0, 0, 1)
            involve(0, 0, first=True)
            involve(1, 1)
            involve(2, 0)
            with eng.Fori(1, GP - 1) as i:
                involve(2 * i + 1, 1)
                involve(2 * i + 2, 0)
            involve(NP - 1, 1, last=True)
            empty_pix(NP - 1, 1, 3 * NP - 1)

        @block.vector
        def _(eng):
            v = nc.vector
            st = Steps(eng, setup)

            def statistics(k, ready, value, src):
                eng.wait_ge(ready, value)
                for n in range(2):
                    v.bn_stats(stats[:, k, n, :], src[:, n * HW:(n + 1) * HW]).then_inc(gn_step, 1)

            for n, t in enumerate((wi[:, :], wr[:, :], wq8[:, :], xhi[:, :, :, :], xlo[:, :, :, :],
                                   whi[:, :, :, :], wlo[:, :, :, :])):
                v.memset(t.bitcast(F32), 0.0).then_inc(zeroed, 1)
            eng.wait_ge(zeroed, ZEROS)
            st.start(0)
            eng.wait_ge(consts_in, CONSTS_IN)
            st.then(v.memset(one[:, :], 1.0))
            st.then(v.scalar_tensor_tensor(sp[:, 0:1], alpha[:, :], -1.0, alpha[:, :], ALU.mult, ALU.max))
            st.then(v.tensor_scalar(rsc[:, 0:1], rpar[:, 4:5], BN_EPS, None, ALU.add))
            st.then(v.memset(mhalf[:, :], -0.5))
            assert st.n == POW_STEP
            st.then(v.tensor_tensor(tmp32[:, 0:2, 0, :], wk_s[:, :].rearrange("p (n d) -> p n d", n=HEADS),
                                    q_s[:, :].rearrange("p (n d) -> p n d", n=HEADS), ALU.mult))
            st.then(v.tensor_reduce(wq[:, :], tmp32[:, 0:2, 0, :], AX.X, ALU.add))
            for part in range(PARTS):
                for n in range(2):
                    p = slice(64 * n, 64 * n + 64)
                    dst = wq8[p, :].rearrange("p (i r) -> p i r", r=AR + 4)[:, :, 32 * part + 2 * n:32 * part + 2 * n + 2]
                    st.then(v.tensor_scalar(dst, wq[p, :].unsqueeze(1).to_broadcast([64, GP, HEADS]),
                                            DH ** -0.5, None, ALU.mult))
            st.then(v.tensor_tensor(
                tmp32[:, :, :, :],
                wv_s[:, :].rearrange("p (n d) -> p n d", n=HEADS).unsqueeze(2).to_broadcast([128, HEADS, K, DH]),
                wm_s[:, :].rearrange("p (n d k) -> p n k d", n=HEADS, d=DH), ALU.mult))
            st.then(v.tensor_reduce(gate[:, :, :], tmp32[:, :, :, :], AX.X, ALU.add))
            st.then(v.tensor_copy(spread_sel[:, :, :].rearrange("p a b -> p (a b)"), st_sel))
            eng.wait_ge(setup_pool, 1)
            st.then(v.tensor_tensor(rsc[:, 1:2], rsc[:, 2:3], rpar[:, 1:2], ALU.mult))
            st.then(v.tensor_tensor(rsc[:, 2:3], rpar[:, 0:1], rpar[:, 3:4], ALU.subtract))
            st.then(v.scalar_tensor_tensor(rsc[:, 3:4], rsc[:, 2:3], rsc[:, 1:2], rpar[:, 2:3], ALU.mult, ALU.add))
            eng.wait_ge(setup_act, 2)
            st.then(v.tensor_scalar(sp[:, 3:4], alpha[:, :], 0.0, sp[:, 2:3], ALU.max, ALU.add))
            st.then(v.tensor_scalar(gain[:, :], sp[:, 3:4], float(S) / HEADS, None, ALU.mult))
            v.memset(allowed[:, :, :, :], 1.0).then_inc(setup_done, 1)

            gn = Steps(eng, gn_step)

            def group_norm(src, lo_k, hi_k, full, value, freed, turn):
                n = hi_k - lo_k
                avg = src.rearrange("p (k s) -> p k s", s=2)
                rows = mv[:, lo_k:hi_k, :]
                eng.wait_ge(full, value)
                gn.then(v.tensor_copy(gnt[:, 0, 0:n], avg[:, :, 0]))
                ins = v.tensor_scalar(gnt[:, 1, 0:n], avg[:, :, 1], GN_EPS, None, ALU.add)
                if freed is None:
                    gn.then(ins)
                else:
                    ins.then_inc(freed[0], 1)
                    eng.wait_ge(freed[0], freed[1])
                gn.then(v.tensor_tensor(gnt[:, 2, 0:n], rows[:, :, 0], gnt[:, 0, 0:n], ALU.subtract))
                gn.then(v.tensor_tensor(gnt[:, 3, 0:n], gnt[:, 2, 0:n], gnt[:, 2, 0:n], ALU.mult))
                gn.then(v.tensor_tensor(gnt[:, 4, 0:n], gnt[:, 3, 0:n], gnt[:, 1, 0:n], ALU.add))
                eng.wait_ge(rstd_ready, turn)
                v.scalar_tensor_tensor(nmr[:, lo_k:hi_k], gnt[:, 0, 0:n], -1.0, rstd[:, lo_k:hi_k],
                                       ALU.mult, ALU.mult).then_inc(nmr_ready, 1)

            def softmax(p, a, g):
                use = Use(p, ("scores",))
                so = Steps(eng, soft_step)
                so.start(SOFT_STEPS * a)
                eng.wait_ge(att_full, use.full)
                so.then(v.tensor_reduce(soft[:, 0:1], att[0:AR, use.unit, :], AX.X, ALU.max))
                v.tensor_scalar(soft[:, 1:2], soft[:, 0:1], -1.0, None, ALU.mult).then_inc(negmax_ready, 1)
                eng.wait_ge(att_free[use.unit], use.freed)
                so.then(v.reciprocal(soft[:, 3:4], soft[:, 2:3]))
                so.then(v.tensor_scalar(attn, attn, soft[:, 3:4], None, ALU.mult))
                so.then(v.tensor_copy(parts[:, g, :], attn))
                so.then(v.tensor_tensor(attn, attn, parts[:, g, :], ALU.subtract))
                so.then(v.tensor_copy(parts[32:64, g, :], attn[32:64, :]))
                so.then(v.tensor_copy(parts[64:AR, g, :], attn[64:AR, :]))
                assert so.n == SOFT_STEPS
                v.tensor_tensor(parts[64:AR, g, :], attn[64:AR, :], parts[64:AR, g, :], ALU.subtract)\
                    .then_inc(parts_ready, 1)

            def pool(p, a, g, i, n):
                use = Use(p, ("spread", i, n))
                if i == 0 and n == 0:
                    eng.wait_ge(parts_ready, a + 1)
                else:
                    before = Use(p, ("spread", i - 1 + n, 1 - n))
                    eng.wait_ge(att_free[before.unit], before.freed)
                eng.wait_ge(att_full, use.full)
                v.scalar_tensor_tensor(work[:, :], att[:, use.unit, :], 1.0, x[:, g * GP + i, :], ALU.mult, ALU.mult,
                                       accum_out=pooled[:, i, n:n + 1]).then_inc(att_free[use.unit], 1)

            def bc(ap, axis, shape):
                return ap.unsqueeze(axis).to_broadcast(shape)

            def route(p, a, g):
                sh = [128, GP, K]
                r = Steps(eng, route_step)
                r.start(ROUTE_STEPS * a)
                for n in range(HEADS):
                    use = Use(p, ("spread", GP - 1, n))
                    eng.wait_ge(att_free[use.unit], use.freed)
                for n in range(HEADS):
                    r.then(v.tensor_tensor(zt[:, n, :, :], bc(pooled[:, :, n], 2, sh), bc(gate[:, n, :], 1, sh), ALU.mult))
                v.tensor_tensor(zt[:, 0, :, :], zt[:, 0, :, :], zt[:, 1, :, :], ALU.add).then_inc(gated_ready, 1)
                use = Use(p, ("logits",))
                eng.wait_ge(att_full, use.full)
                ok = allowed[:, g, :, :]
                v.tensor_tensor(rt[:, 0, :, :], att[:, use.unit, 0:GP * K].rearrange("p (i k) -> p i k", k=K), ok,
                                ALU.mult).then_inc(att_free[use.unit], 1)
                eng.wait_ge(att_free[use.unit], use.freed)
                r.then(v.tensor_scalar(rt[:, 1, :, :], ok, -1.0, 1e9, ALU.add, ALU.mult))
                r.then(v.tensor_tensor(rt[:, 0, :, :], rt[:, 0, :, :], rt[:, 1, :, :], ALU.add))
                r.then(v.tensor_reduce(rs[:, 0, :], rt[:, 0, :, :], AX.X, ALU.max))
                v.tensor_tensor(rt[:, 2, :, :], rt[:, 0, :, :], bc(rs[:, 0, :], 2, sh), ALU.subtract)\
                    .then_inc(shifted_ready, 1)
                eng.wait_ge(rexp_ready, a + 1)
                r.then(v.tensor_reduce(rs[:, 1, :], rt[:, 3, :, :], AX.X, ALU.add))
                r.then(v.reciprocal(rs[:, 2, :], rs[:, 1, :]))
                w = rt[:, 4, :, :]
                r.then(v.tensor_tensor(w, rt[:, 3, :, :], bc(rs[:, 2, :], 2, sh), ALU.mult))
                full = [128, GP, K, K]
                wj, we = bc(w, 2, full), bc(w, 3, full)
                r.then(v.tensor_tensor(cmp[:, 0, :, :, :], wj, we, ALU.is_gt))
                r.then(v.tensor_tensor(cmp[:, 1, :, :, :], wj, we, ALU.is_equal))
                r.then(v.tensor_tensor(cmp[:, 2, :, :, :], cmp[:, 1, :, :, :], bc(earlier[:, :, :], 1, full), ALU.mult))
                r.then(v.tensor_tensor(cmp[:, 1, :, :, :], cmp[:, 2, :, :, :], cmp[:, 0, :, :, :], ALU.add))
                r.then(v.tensor_reduce(rt[:, 5, :, :], cmp[:, 1, :, :, :], AX.X, ALU.add))
                r.then(v.tensor_scalar(rt[:, 6, :, :], rt[:, 5, :, :], 1.5, None, ALU.is_lt))
                r.then(v.tensor_tensor(rt[:, 7, :, :], w, rt[:, 6, :, :], ALU.mult))
                r.then(v.tensor_reduce(rs[:, 3, :], rt[:, 7, :, :], AX.X, ALU.add))
                r.then(v.tensor_scalar(rs[:, 4, :], rs[:, 3, :], 1e-9, None, ALU.add))
                r.then(v.reciprocal(rs[:, 5, :], rs[:, 4, :]))
                r.then(v.tensor_tensor(wsel[:, :, :], rt[:, 7, :, :], bc(rs[:, 5, :], 2, sh), ALU.mult))
                r.then(v.tensor_scalar(rt[:, 8, :, :], rt[:, 5, :, :], 0.5, None, ALU.is_lt))
                some = allowed[:, g, :, 0:K - 1]
                r.then(v.tensor_tensor(rt[:, 9, :, 0:K - 1], some, rt[:, 8, :, 0:K - 1], ALU.subtract))
                r.then(v.tensor_scalar(some, rt[:, 9, :, 0:K - 1], 0.0, 1.0, ALU.max, ALU.min))
                r.then(v.tensor_tensor(rt[:, 10, :, :], wsel[:, :, :], bc(be_s[:, :], 1, sh), ALU.mult))
                assert r.n == ROUTE_STEPS
                v.tensor_reduce(bias[:, bass.ds(g * GP, GP)] if not isinstance(g, int) else bias[:, g * GP:(g + 1) * GP],
                                rt[:, 10, :, :], AX.X, ALU.add).then_inc(bias_ready, 1)

            def modulate(p, g, i, q):
                use = Use(p, ("map", i))
                eng.wait_ge(att_free[use.unit], use.freed)
                v.tensor_tensor(xm[:, :], xm[:, :], x[:, g * GP + i, :], ALU.mult).then_inc(xm_ready, 1)

            def combine(i, q):
                if not (isinstance(q, int) and q == 0):
                    eng.wait_ge(wlo_ready, 2 * q)
                cflat = comb[:, :, :].rearrange("p a b -> p (a b)")
                v.tensor_scalar(cflat, experts[:, 0, :], wsel[:, i, 0:1], None, ALU.mult).then_inc(comb_step, 1)
                for e in range(1, K):
                    eng.wait_ge(comb_step, K * q + e)
                    v.scalar_tensor_tensor(cflat, experts[:, e, :], wsel[:, i, e:e + 1], cflat, ALU.mult, ALU.add)\
                        .then_inc(comb_step, 1)

            def channel_stats(g):
                for k in range(g * GP, (g + 1) * GP):
                    use = Use(-1, ("turn", k))
                    eng.wait_ge(att_free[use.unit], use.freed)
                    for n in range(2):
                        gn.then(v.bn_stats(stats[:, k, n, :], xin[:, k, n * HW:(n + 1) * HW]))
                    v.bn_aggr(mv[:, k, :], stats[:, k, :, :]).then_inc(mv_ready, 1)

            gn.start(0)
            channel_stats(0)
            use = Use(-1, ("gn", 0))
            group_norm(att[:, use.unit, 0:2 * GP], 0, GP, att_full, use.full, (att_free[use.unit], use.freed), 1)
            softmax(-1, 0, 0)
            for i in range(GP):
                for n in range(HEADS):
                    pool(-1, 0, 0, i, n)
            route(-1, 0, 0)
            channel_stats(1)
            use = Use(-1, ("gn", 1))
            group_norm(att[:, use.unit, 0:2 * GP], GP, NP, att_full, use.full, (att_free[use.unit], use.freed), 2)
            modulate(-1, 0, 0, 0)
            combine(0, 0)

            def phase(p, g, ng, attend):
                for j in range(GP):
                    q = p * GP + j
                    if j < GP - 1:
                        modulate(p, g, j + 1, q + 1)
                        combine(j + 1, q + 1)
                    elif attend:
                        modulate(p, ng, 0, q + 1)
                        combine(0, q + 1)
                    if attend:
                        if j == 0:
                            softmax(p, p + 1, ng)
                        for key, _ in slot_uses(j):
                            if key[0] == "spread":
                                pool(p, p + 1, ng, key[1], key[2])
                        if j == 6:
                            route(p, p + 1, ng)

            with eng.Fori(0, PHASES - 1) as p:
                g = eng.snap(p % 2)
                ng = eng.snap((p + 1) % 2)
                phase(p, g, ng, True)
            phase(PHASES - 1, (PHASES - 1) % 2, None, False)

            GN_BASE = gn.n
            with eng.Fori(0, NP) as k:
                eng.wait_ge(x_ready, NP + GP * (PHASES - 2) + k + 1)
                v.tensor_tensor(xin[:, k, :], xin[:, k, :], x[:, k, :], ALU.add).then_inc(x1_step, 1)
                eng.wait_ge(x1_step, k + 1)
                gn.start(GN_BASE + 2 * k)
                for n in range(2):
                    gn.then(v.bn_stats(stats[:, k, n, :], xin[:, k, n * HW:(n + 1) * HW]))
            for k in range(NP):
                v.bn_aggr(mv[:, k, :], stats[:, k, :, :]).then_inc(mv2_ready, 1)
            eng.wait_ge(mv2_ready, NP)
            for n in range(2):
                v.memset(xip[n], 0.0).then_inc(pads_zeroed, 1)
                v.memset(rstk[n][AR:RR, :].bitcast(F32), 1.0).then_inc(pads_zeroed, 1)
            eng.wait_ge(pads_zeroed, 4)
            late = Steps(eng, late_setup)
            eng.wait_ge(late_consts_in, 16 * len(LATE_CONSTS))
            late.then(v.tensor_copy(sum_sel[:, :, :].rearrange("p a b -> p (a b)"), st_sum))
            late.then(v.tensor_copy(
                st_exp.rearrange("p (g j t) -> p g j t", g=G16, j=C // G16),
                st_ws.rearrange("p (g t) -> p g t", g=G16).unsqueeze(2).to_broadcast([RR, G16, C // G16, TAPS])))
            for n in range(2):
                late.then(v.tensor_scalar(st_bd[:, :, 64 * n:64 * n + 64], st_exp.rearrange("p (t c) -> p t c", t=TAPS),
                                        masks[:, n:n + 1], None, ALU.mult))
            hi_of = wse[:, :, :].rearrange("p a b -> p (a b)")
            bd = st_bd.rearrange("p t c -> p (t c)")
            late.then(v.tensor_copy(hi_of, bd))
            late.then(v.tensor_tensor(bd, bd, hi_of.bitcast(F32), ALU.subtract))
            late.then(v.tensor_scalar(bd, bd, masks[:, 2:3], None, ALU.mult))
            v.scalar_tensor_tensor(hi_of, hi_of.bitcast(F32), masks[:, 3:4], bd, ALU.mult, ALU.add).then_inc(wse_ready, 1)
            gn.start(GN_BASE + 2 * NP)
            group_norm(att[:, 1, 0:2 * NP], 0, NP, gn2_full, 1, None, 3)

            def product(k, s, kk, first, second):
                e = k * TAPS + kk
                unit = (s * TAPS + kk) % 2
                slot = kk % RING
                kh, kw = divmod(kk, 3)
                eng.wait_ge(exp_full, e + 1)
                if kk == 0:
                    eng.wait_ge(misc_free, 1 if first else 3 if second else 3 * k - 1)
                old = (kk - RING) % TAPS
                ok_ = k if kk >= RING else k - 1
                if not (first and kk < RING):
                    if old == DIRECT:
                        eng.wait_ge(sum_done, ok_ * TAPS + old + 1)
                    elif old in LO_POOL:
                        eng.wait_ge(lo_pool_ready, ok_ * len(LO_POOL) + LO_POOL.index(old) + 1)
                    else:
                        eng.wait_ge(lo_dve_ready, ok_ * len(LO_DVE) + LO_DVE.index(old) + 1)
                v.tensor_tensor(img(prod[slot]), img(conv[:, unit, :]), xip[s][:, kh:kh + H, kw:kw + W], ALU.mult)\
                    .then_inc(prod_ready, 1)

            def split_lo(k, kk):
                slot = kk % RING
                eng.wait_ge(hi_ready, k * len(SPLIT) + SPLIT.index(kk) + 1)
                v.tensor_tensor(lo[slot], prod[slot], hi[slot].bitcast(F32), ALU.subtract).then_inc(lo_dve_ready, 1)

            def finish(k, m):
                eng.wait_ge(sum_done, TAPS * (k + 1))
                if m is not None:
                    eng.wait_ge(misc_full, m)
                v.tensor_tensor(fin, att[:, 0, :], xin[:, k, :], ALU.add).then_inc(fin_ready, 1)

            def involve(k, s, first=False, second=False):
                for kk in range(TAPS):
                    product(k, s, kk, first, second)
                    if kk - 1 in LO_DVE:
                        split_lo(k, kk - 1)
                    if kk == 2 and not first:
                        finish(k - 1, None if second else 3 * k + 1)

            involve(0, 0, first=True)
            involve(1, 1, second=True)
            involve(2, 0)
            with eng.Fori(1, GP - 1) as i:
                involve(2 * i + 1, 1)
                involve(2 * i + 2, 0)
            involve(NP - 1, 1)
            finish(NP - 1, 3 * NP - 1)

        @block.gpsimd
        def _(eng):
            v = nc.gpsimd
            eng.wait_ge(setup, POW_STEP)
            v.tensor_tensor(rsc[:, 2:3], rsc[:, 0:1], mhalf[0:AR, 0:1], ALU.pow).then_inc(setup_pool, 1)

            def inverse_root(step, lo_k, hi_k):
                n = hi_k - lo_k
                eng.wait_ge(gn_step, step)
                v.tensor_tensor(rstd[:, lo_k:hi_k], gnt[:, 4, 0:n], mhalf[:, 0:n], ALU.pow).then_inc(rstd_ready, 1)

            def split_lo(q, s):
                eng.wait_ge(whi_ready, 2 * q + 2)
                if isinstance(q, int) and q == 0:
                    eng.wait_ge(rstd_ready, 2)
                else:
                    eng.wait_ge(xlo_ready, q)
                for n in range(2):
                    p = slice(64 * n, 64 * n + 64)
                    v.tensor_tensor(wlo[p, s, :, 64 * n:64 * n + 64], comb[p, :, :],
                                    whi[p, s, :, 64 * n:64 * n + 64].bitcast(F32), ALU.subtract).then_inc(wlo_ready, 1)
                    eng.wait_ge(wlo_ready, 2 * q + n + 1)
                eng.wait_ge(xhi_ready, q + 1)
                v.tensor_tensor(inner(xlo, s), img(xm[:, :]), inner(xhi, s).bitcast(F32), ALU.subtract)\
                    .then_inc(xlo_ready, 1)

            per_group = 2 * GP + 4
            inverse_root(per_group, 0, GP)
            inverse_root(2 * per_group, GP, NP)
            split_lo(0, 0)
            with eng.Fori(0, PHASES - 1) as p:
                for j in range(GP):
                    split_lo(p * GP + j + 1, (j + 1) % 2)
            for j in range(GP - 1):
                split_lo((PHASES - 1) * GP + j + 1, (j + 1) % 2)

            eng.wait_ge(xlo_ready, PHASES * GP)
            inverse_root(2 * per_group + 2 * NP + 5, 0, NP)

            def r_lo(k, s):
                if isinstance(k, int) and k == 0:
                    eng.wait_ge(rstd_ready, 3)
                else:
                    eng.wait_ge(lo_pool_ready, (k - 1) * len(LO_POOL) + LO_POOL.index(5) + 1)
                eng.wait_ge(rhi_ready, k + 1)
                v.tensor_tensor(rstk[s][32:64, :], r96[32:64, :], rstk[s][32:64, :].bitcast(F32), ALU.subtract)\
                    .then_inc(rstk_ready, 1)
                eng.wait_ge(rstk_ready, k + 1)

            def involve(k, s, last=False):
                for kk in range(TAPS):
                    slot = kk % RING
                    if kk in LO_POOL:
                        eng.wait_ge(hi_ready, k * len(SPLIT) + SPLIT.index(kk) + 1)
                        v.tensor_tensor(lo[slot], prod[slot], hi[slot].bitcast(F32), ALU.subtract)\
                            .then_inc(lo_pool_ready, 1)
                    if kk == 5 and not last:
                        r_lo(k + 1, 1 - s)

            r_lo(0, 0)
            with eng.Fori(0, GP - 1) as i:
                involve(2 * i, 0)
                involve(2 * i + 1, 1)
            involve(NP - 2, 0)
            involve(NP - 1, 1, last=True)


def constants():
    rows = np.arange(AR)
    spread = np.zeros((AR, GP, 3, 128), np.float32)
    for i in range(GP):
        for image in range(2):
            for head in range(HEADS):
                hit = rows % 32 == 4 * i + 2 * image + head
                spread[hit, i, head, 64 * image:64 * image + 64] = 1
                spread[hit, i, 2, 64 * image:64 * image + 64] = 1
    ch = np.arange(128)
    total = np.zeros((128, TAPS, 128), np.float32)
    for t in range(TAPS):
        for c in range(C):
            for image in range(2):
                total[64 * image + c, t, 64 * image + (t * C + c) // TAPS] = 1
    row = np.arange(RR)
    low = ((row >= 64) & (row < 96)) | (row == 97)
    masks = np.stack([(row % 32 < CR) | (row >= AR), (row % 32 >= CR) | (row >= AR), low, ~low], 1).astype(np.float32)
    return {
        "c_spread": spread.reshape(AR, -1),
        "c_ident": np.eye(128, dtype=np.float32),
        "c_pair": np.where(ch[:, None] // 2 == ch // 2, 0.5, 0).astype(np.float32),
        "c_same": (ch[:, None] // 64 == ch // 64).astype(np.float32),
        "c_sum": total.reshape(128, -1),
        "c_masks": masks,
        "c_earlier": np.tril(np.ones((K, K), np.float32), -1).reshape(1, -1)[0],
    }


def kernel(**inputs):
    import concourse.bacc as bacc
    from concourse.bass_utils import run_bass_kernel_spmd

    a = {n: np.ascontiguousarray(v) for n, v in inputs.items()}
    arrays = {
        "x": a["x"].reshape(B, S, C),
        "q": a["L0_conv_q"].reshape(D), "Wk": a["L0_conv_Wk"], "Wv": a["L0_conv_Wv"],
        "Wmlp": a["L0_conv_Wmlp"].reshape(D * K), "alpha": a["L0_conv_alpha"].reshape(1),
        "We": a["L0_conv_We"].reshape(K * TAPS, C, C), "be": np.ascontiguousarray(a["L0_conv_be"].T),
        "rpar": np.ascontiguousarray(np.tile(np.stack(
            [a["L1_conv_" + n] for n in ("br", "gamma", "beta", "mean", "var")], 1), (2 * PARTS, 1))),
        "Wr": a["L1_conv_Wr"], "Ws": a["L1_conv_Ws"], "bs": a["L1_conv_bs"], "Wi": a["L1_conv_Wi"],
        "bi": a["L1_conv_bi"].reshape(C, 1),
        **constants(),
    }
    nc = bacc.Bacc("TRN2", target_bir_lowering=False, num_devices=1)
    A = {n: nc.dram_tensor("in_" + n, v.shape, mybir.dt.from_np(v.dtype), kind="ExternalInput").ap()
         for n, v in arrays.items()}
    out = nc.dram_tensor("out", (B, S, C), F32, kind="ExternalOutput").ap()
    build(nc, A, out)
    r = run_bass_kernel_spmd(nc, [{"in_" + n: v for n, v in arrays.items()}], core_ids=[0])
    return r.results[0]["out"].reshape(B, H, W, C)
```

```python
from contextlib import ExitStack

import numpy as np

import concourse.bass as bass
from concourse import mybir

F32 = mybir.dt.float32
F32R = mybir.dt.float32r
BF16 = mybir.dt.bfloat16
ALU = mybir.AluOpType
ACT = mybir.ActivationFunctionType
AX = mybir.AxisListType

B, H, W, C = 32, 32, 32, 64
S = H * W
NP = B // 2
GP = NP // 2
HW = S // 2
PW = W + 2
PS = PW * PW
K = 4
HEADS, DH = 2, 16
D = HEADS * DH
STEPS = 3
PHASES = 2 * STEPS
TEMP = 1.5
TAPS = 9
CR = 16
G16 = 16
GN_EPS = 1e-5
BN_EPS = 1e-3
PARTS = 3
AR = PARTS * 4 * GP
RR = 98
T = S // 128

CH = 4
PROLOGUE_USES = (
    [("turn", k) for k in range(CH)] + [("gn", 0)] + [("turn", k) for k in range(CH, GP)] + [("gn", 1), ("scores",)]
    + [u for i in range(CH) for u in (("spread", i, 0), ("spread", i, 1), ("turn", GP + i))] + [("gn", 2)]
    + [u for i in range(CH, GP) for u in (("spread", i, 0), ("spread", i, 1), ("turn", GP + i))]
    + [("logits",), ("map", 0), ("gn", 3)]
)


def slot_uses(j, last=False):
    if last:
        return [(("map", j + 1), 0)] if j < GP - 1 else [(("gn", 4), 6)]
    uses = [(("map", (j + 1) % GP), 0)]
    if j == 0:
        uses += [(("scores",), 6)]
    if 2 <= j <= 5:
        uses += [(("spread", 2 * (j - 2) + m // 2, m % 2), 1 + 2 * m) for m in range(4)]
    if j == 6:
        uses += [(("logits",), 2)]
    return uses


PHASE_USES = [key for j in range(GP) for key, _ in slot_uses(j)]
LAST_USES = [key for j in range(GP) for key, _ in slot_uses(j, True)]
assert len(PHASE_USES) % 2 == 0
RESIDUAL = [k for j in range(GP) for k in ([j] if j < 2 else [j, GP + j - 2])] + [NP - 2, NP - 1]


class Use:

    def __init__(self, p, key):
        if isinstance(p, int) and p == -1:
            at = PROLOGUE_USES.index(key)
            self.unit, self.before, self.full = at % 2, at // 2, at + 1
        elif isinstance(p, int) and p == PHASES - 1:
            at = len(PROLOGUE_USES) + p * len(PHASE_USES) + LAST_USES.index(key)
            self.unit, self.before, self.full = at % 2, at // 2, at + 1
        else:
            at = len(PROLOGUE_USES) + PHASE_USES.index(key)
            self.unit = at % 2
            self.before = p * (len(PHASE_USES) // 2) + at // 2
            self.full = p * len(PHASE_USES) + at + 1
        self.freed = self.before + 1


class Steps:

    def __init__(self, eng, sem):
        self.eng, self.sem, self.base, self.n = eng, sem, 0, 0

    def start(self, base):
        self.base, self.n = base, 0

    def then(self, instruction):
        self.n += 1
        instruction.then_inc(self.sem, 1)
        self.eng.wait_ge(self.sem, self.base + self.n)


BF16_ONE = 0x3F80
SOFT_STEPS, ROUTE_STEPS = 7, 23
POW_STEP = 3
DIRECT = 4
LO_DVE = (1, 3, 6)
LO_POOL = tuple(t for t in range(TAPS) if t != DIRECT and t not in LO_DVE)
SPLIT = tuple(t for t in range(TAPS) if t != DIRECT)
PRODS = 6
RING = 4
R_AFTER = 5
LAG = 4
assert 2 * TAPS % PRODS == 0 and len(SPLIT) % RING == 0


def build(nc, A, out):
    ctx = ExitStack()
    with ctx:
        def sb(name, shape, dt=F32):
            return ctx.enter_context(nc.sbuf_tensor(name, shape, dt))

        def sem(name):
            return ctx.enter_context(nc.semaphore(name))

        xin = sb("xin", [128, NP, S])
        x = sb("x", [128, NP, S])
        with ExitStack() as routed_only:
            experts = routed_only.enter_context(nc.sbuf_tensor("experts", [128, K, TAPS * C], F32))
            work = routed_only.enter_context(nc.sbuf_tensor("work", [128, S], F32))
            parts = routed_only.enter_context(nc.sbuf_tensor("parts", [AR, 2, S], BF16))
        attn = work[0:AR, :]
        sum_sel = sb("sum_sel", [128, TAPS, 128], F32R)
        wse = sb("wse", [RR, TAPS, 128], F32R)
        rstack = sb("rstack", [128, 2, S], F32R)
        comb = sb("comb", [128, TAPS, C])
        whi = sb("whi", [128, 2, TAPS, 128], F32R)
        wlo = sb("wlo", [128, 2, TAPS, 128], F32R)
        xhi = sb("xhi", [128, 2, PW, PW], F32R)
        xlo = sb("xlo", [128, 2, PW, PW], F32R)
        xm = sb("xm", [128, S])
        spread_sel = sb("spread_sel", [AR, GP * 3, 128], BF16)
        ident = sb("ident", [128, 128])
        pair_avg = sb("pair_avg", [128, 128])
        same_image = sb("same_image", [128, 128])
        wi = sb("wi", [128, 128])
        wr = sb("wr", [128, AR])
        wq8 = sb("wq8", [128, 800])
        wk_s = sb("wk_s", [128, D])
        q_s = sb("q_s", [128, D])
        wv_s = sb("wv_s", [128, D])
        wm_s = sb("wm_s", [128, D * K])
        tmp32 = sb("tmp32", [128, HEADS, K, DH])
        wq = sb("wq", [128, HEADS])
        gate = sb("gate", [128, HEADS, K])
        be_s = sb("be_s", [128, K])
        earlier = sb("earlier", [128, K, K])
        alpha = sb("alpha", [128, 1])
        sp = sb("sp", [128, 4])
        gain = sb("gain", [128, 1])
        one = sb("one", [128, 1])
        mhalf = sb("mhalf", [128, 2 * NP])
        masks = sb("masks", [RR, 4])
        rpar = sb("rpar", [AR, 5])
        rsc = sb("rsc", [AR, 4])
        bi_s = sb("bi_s", [128, 1])
        stats = sb("stats", [128, NP, 2, 6])
        mv = sb("mv", [128, NP, 2])
        gnt = sb("gnt", [128, 4, NP])
        negmean = sb("negmean", [128, NP])
        variance = sb("variance", [128, NP])
        rstd = sb("rstd", [128, NP])
        nmr = sb("nmr", [128, NP])
        soft = sb("soft", [AR, 4])
        pooled = sb("pooled", [128, GP, HEADS])
        zt = sb("zt", [128, 2, GP, K])
        rt = sb("rt", [128, 12, GP, K])
        rs = sb("rs", [128, 6, GP])
        cmp = sb("cmp", [128, 3, GP, K, K])
        wsel = sb("wsel", [128, GP, K])
        allowed = sb("allowed", [128, 2, GP, K])
        bias = sb("bias", [128, NP])

        xpix = [x[:, GP + n, :].rearrange("p (t c) -> p t c", t=T) for n in range(GP)]
        stage = x[:, 0:3, :].rearrange("p a b -> p (a b)")
        st_sum = stage[:, 0:TAPS * 128]
        st_ws = stage[0:RR, 1152:1152 + TAPS * G16]
        st_exp = stage[0:RR, 1296:1296 + TAPS * C]
        st_bd = stage[0:RR, 1872:1872 + TAPS * 128].rearrange("p (t c) -> p t c", t=TAPS)

        conv = ctx.enter_context(nc.psum_tensor("conv", [128, 2, S], F32))
        att = ctx.enter_context(nc.psum_tensor("att", [128, 2, S], F32))

        consts_in = sem("consts_in")
        late_consts_in = sem("late_consts_in")
        late_setup = sem("late_setup")
        wse_ready = sem("wse_ready")
        pix_in = [sem(f"pix_in{n}") for n in range(GP)]
        turn_consts_in = sem("turn_consts_in")
        pads_in = sem("pads_in")
        variance_ready = sem("variance_ready")
        inverse_ready = sem("inverse_ready")
        zeroed = sem("zeroed")
        setup = sem("setup")
        setup_pool = sem("setup_pool")
        setup_act = sem("setup_act")
        setup_done = sem("setup_done")
        att_full = sem("att_full")
        att_free = [sem("att_free0"), sem("att_free1")]
        gn_step = sem("gn_step")
        nmr_ready = sem("nmr_ready")
        x_ready = sem("x_ready")
        soft_step = sem("soft_step")
        negmax_ready = sem("negmax_ready")
        exp_ready = sem("exp_ready")
        parts_ready = sem("parts_ready")
        gated_ready = sem("gated_ready")
        route_step = sem("route_step")
        shifted_ready = sem("shifted_ready")
        rexp_ready = sem("rexp_ready")
        bias_ready = sem("bias_ready")
        xm_ready = sem("xm_ready")
        xhi_ready = sem("xhi_ready")
        xlo_ready = sem("xlo_ready")
        comb_step = sem("comb_step")
        whi_ready = sem("whi_ready")
        wlo_ready = sem("wlo_ready")
        conv_full = sem("conv_full")
        x1_step = sem("x1_step")
        mv_ready = sem("mv_ready")
        pads_zeroed = sem("pads_zeroed")
        misc_full = sem("misc_full")
        misc_free = sem("misc_free")
        xn_ready = sem("xn_ready")
        xi_ready = sem("xi_ready")
        r_ready = sem("r_ready")
        rhi_ready = sem("rhi_ready")
        rstk_ready = sem("rstk_ready")
        exp_full = sem("exp_full")
        prod_ready = sem("prod_ready")
        hi_ready = sem("hi_ready")
        lo_dve_ready = sem("lo_dve_ready")
        lo_pool_ready = sem("lo_pool_ready")
        sum_done = sem("sum_done")
        fin_ready = sem("fin_ready")
        stored = [sem("stored0"), sem("stored1")]

        flat = x[:, :, :].rearrange("p a b -> p (a b)")
        prod = [flat[:, n * S:(n + 1) * S] for n in range(PRODS)]
        xn = [flat[:, (6 + n) * S:(7 + n) * S] for n in range(2)]
        r96 = flat[0:AR, 8 * S:9 * S]
        xip = [flat[:, 9 * S + n * PS:9 * S + (n + 1) * PS].rearrange("p (a b) -> p a b", a=PW)
               for n in range(2)]
        fin = flat[:, 12 * S:13 * S]
        pix = [flat[:, (13 + n) * S:(14 + n) * S].rearrange("p (t c) -> p t c", t=T) for n in range(2)]

        def pad_flat(t, n):
            return t[:, n, :, :].rearrange("p a b -> p (a b)")[:, 0:S]

        hi = [pad_flat(t, n) for t in (xhi, whi) for n in range(2)]
        lo = [pad_flat(t, n) for t in (xlo, wlo) for n in range(2)]
        rstk = [rstack[:, n, :] for n in range(2)]

        def prod_slot(s, kk):
            return (s * TAPS + kk) % PRODS

        def img(ap):
            return ap.rearrange("p (a b) -> p a b", a=H)

        def inner(padded, n):
            return padded[:, n, 1:H + 1, 1:W + 1]

        def halves():
            return ((h, slice(h * HW, (h + 1) * HW)) for h in range(2))

        CONSTS = [
            (spread_sel[:, :, :].rearrange("p a b -> p (a b)").bitcast(mybir.dt.uint16), A["c_spread"]),
            (same_image[:, :], A["c_same"]), (masks[:, :], A["c_masks"]),
            (earlier[:, :, :].rearrange("p a b -> p (a b)"), A["c_earlier"].partition_broadcast(128)),
            (q_s[:, :], A["q"].partition_broadcast(128)),
            (wm_s[:, :], A["Wmlp"].partition_broadcast(128)),
            (alpha[:, :], A["alpha"].partition_broadcast(128)),
            (rpar[:, :], A["rpar"]),
        ]
        for n in range(2):
            p = slice(64 * n, 64 * n + 64)
            CONSTS += [
                (wk_s[p, :], A["Wk"]), (wv_s[p, :], A["Wv"]), (be_s[p, :], A["be"]),
                (experts[p, :, :].rearrange("p k (t c) -> p (k t) c", t=TAPS), A["We"].rearrange("t i o -> i t o")),
                (bi_s[p, :], A["bi"]),
            ]
        LATE_CONSTS = [(st_sum, A["c_sum"]), (st_ws[AR:RR, :], A["bs"].partition_broadcast(2))]
        LATE_CONSTS += [(st_ws[CR * a:CR * a + CR, :], A["Ws"]) for a in range(2 * PARTS)]
        BLOCKS = [(wi[64 * n:64 * n + 64, 64 * n:64 * n + 64], A["Wi"]) for n in range(2)]
        BLOCKS += [(wr[64 * n:64 * n + 64, 32 * a + CR * n:32 * a + CR * n + CR], A["Wr"])
                   for n in range(2) for a in range(PARTS)]
        CONSTS_IN = 16 * (len(CONSTS) + len(BLOCKS))
        ZEROS = 3

        block = ctx.enter_context(nc.Block())

        @block.sync
        def _(eng):
            def load_pair(k, n):
                for m in range(2):
                    eng.dma_start(xpix[n][:, :, 64 * m:64 * m + 64],
                                  A["x"][2 * k + m, :, :].rearrange("(p t) c -> p t c", t=T)).then_inc(pix_in[n], 16)

            for k in range(GP):
                load_pair(k, k)
            eng.wait_ge(zeroed, ZEROS)
            for dst, src in BLOCKS:
                eng.dma_start(dst, src).then_inc(consts_in, 16)
            for n in range(GP):
                use = Use(-1, ("turn", n))
                eng.wait_ge(att_free[use.unit], use.freed)
                load_pair(GP + n, n)
            eng.wait_ge(x1_step, RESIDUAL.index(2) + 1)
            for dst, src in LATE_CONSTS:
                eng.dma_start(dst, src).then_inc(late_consts_in, 16)

            def store_pair(k, n, uses):
                eng.wait_ge(misc_free, uses)
                for m in range(2):
                    eng.dma_start(out[2 * k + m, :, :].rearrange("(p t) c -> p t c", t=T),
                                  pix[n][:, :, 64 * m:64 * m + 64]).then_inc(stored[n], 16)

            with eng.Fori(0, GP - 1) as i:
                for n in range(2):
                    store_pair(2 * i + n, n, 6 * i + 3 * n + 8)
            for n in range(2):
                store_pair(NP - 2 + n, n, 3 * NP + n)
            for n in range(2):
                eng.wait_ge(stored[n], 2 * 16 * GP)

        @block.tensor
        def _(eng):
            def claim(use):
                if not (isinstance(use.before, int) and use.before == 0):
                    eng.wait_ge(att_free[use.unit], use.before)

            def turn(k):
                use = Use(-1, ("turn", k))
                claim(use)
                eng.wait_ge(pix_in[k % GP], 32 * (k // GP + 1))
                for t in range(T):
                    last = nc.tensor.transpose(att[:, use.unit, 128 * t:128 * t + 128], xpix[k % GP][:, t, :], ident[:, :])
                last.then_inc(att_full, 1)

            def group_average(p, c, lo_k, hi_k, value):
                use = Use(p, ("gn", c))
                claim(use)
                eng.wait_ge(mv_ready, value)
                nc.tensor.matmul(att[:, use.unit, 0:2 * (hi_k - lo_k)], pair_avg[:, :], mv[:, lo_k:hi_k, :],
                                 start=True, stop=True).then_inc(att_full, 1)

            def scores(p, a, g):
                use = Use(p, ("scores",))
                claim(use)
                prologue = isinstance(a, int) and a == 0
                if not prologue:
                    eng.wait_ge(x_ready, NP + GP * p)
                for i in range(GP):
                    if prologue:
                        eng.wait_ge(x_ready, i + 1)
                    for h, cols in halves():
                        last = nc.tensor.matmul(att[0:AR, use.unit, cols], wq8[:, AR * i:AR * i + AR],
                                                x[:, g * GP + i, cols], start=(i == 0), stop=(i == GP - 1))
                last.then_inc(att_full, 1)

            def spread(p, a, g, i, n):
                use = Use(p, ("spread", i, n))
                claim(use)
                if i == 0 and n == 0:
                    eng.wait_ge(parts_ready, a + 1)
                for h, cols in halves():
                    last = nc.tensor.matmul(att[:, use.unit, cols], spread_sel[:, 3 * i + n, :], parts[:, g, cols],
                                            start=True, stop=True)
                last.then_inc(att_full, 1)

            def attention_map(p, g, i):
                use = Use(p, ("map", i))
                claim(use)
                for h, cols in halves():
                    last = nc.tensor.matmul(att[:, use.unit, cols], spread_sel[:, 3 * i + 2, :], parts[:, g, cols],
                                            start=True, stop=True)
                last.then_inc(att_full, 1)

            def logits(p, a):
                use = Use(p, ("logits",))
                claim(use)
                eng.wait_ge(gated_ready, a + 1)
                nc.tensor.matmul(att[:, use.unit, 0:GP * K], same_image[:, :],
                                 zt[:, 0, :, :], start=True, stop=True).then_inc(att_full, 1)

            def convolve(p, j, a, g, final=False):
                q = p * GP + j
                s = j % 2
                eng.wait_ge(xlo_ready, q + 1)
                eng.wait_ge(wlo_ready, 2 * q + 2)
                eng.wait_ge(x_ready, NP + q - 1)
                for t in range(TAPS):
                    kh, kw = divmod(t, 3)
                    for wt, xt in ((whi, xhi), (whi, xlo), (wlo, xhi)):
                        for h, cols in halves():
                            last = nc.tensor.matmul(
                                conv[:, s, cols], wt[:, s, t, :],
                                xt[:, s, kh + 16 * h:kh + 16 * h + 16, kw:kw + W],
                                start=(t == 0 and wt is whi and xt is xhi), stop=(t == TAPS - 1 and wt is wlo))
                    if t == TAPS - 1:
                        last.then_inc(conv_full, 1)
                    for key, behind in slot_uses(j, final):
                        if behind == t:
                            if key[0] == "map":
                                attention_map(p, a[1] if key[1] == 0 else g, key[1])
                            elif key[0] == "gn":
                                group_average(p, 4, 0, GP, NP + RESIDUAL.index(GP - 1) + 1)
                            elif key[0] == "scores":
                                scores(p, a[0], a[1])
                            elif key[0] == "spread":
                                spread(p, a[0], a[1], key[1], key[2])
                            elif key[0] == "logits":
                                logits(p, a[0])

            eng.wait_ge(turn_consts_in, 32)
            for key in PROLOGUE_USES:
                if key[0] == "turn":
                    turn(key[1])
                elif key[0] == "gn":
                    group_average(-1, key[1], CH * key[1], CH * key[1] + CH, CH * key[1] + CH)
                elif key[0] == "scores":
                    eng.wait_ge(setup_done, 1)
                    scores(-1, 0, 0)
                elif key[0] == "spread":
                    spread(-1, 0, 0, key[1], key[2])
                elif key[0] == "logits":
                    logits(-1, 0)
                else:
                    attention_map(-1, 0, 0)
            with eng.Fori(0, PHASES - 1) as p:
                g = eng.snap(p % 2)
                ng = eng.snap((p + 1) % 2)
                for j in range(GP):
                    convolve(p, j, (p + 1, ng), g)
            for j in range(GP):
                convolve(PHASES - 1, j, None, (PHASES - 1) % 2, final=True)

            def project(k, s, m, weights, rows):
                if not (isinstance(m, int) and m == 0):
                    eng.wait_ge(misc_free, m)
                eng.wait_ge(xn_ready, k + 1)
                for h, cols in halves():
                    last = nc.tensor.matmul(att[0:rows, 1, cols], weights, xn[s][:, cols], start=True, stop=True)
                last.then_inc(misc_full, 1)

            def turn_back(k, m):
                eng.wait_ge(misc_free, m)
                eng.wait_ge(fin_ready, k + 1)
                cols = fin.rearrange("c (p t) -> c t p", t=T)
                for t in range(T):
                    last = nc.tensor.transpose(att[:, 1, 128 * t:128 * t + 128], cols[:, t, :], ident[:, :])
                last.then_inc(misc_full, 1)

            def expand(k, s, kk):
                e = k * TAPS + kk
                unit = (s * TAPS + kk) % 2
                if kk == 0:
                    eng.wait_ge(rstk_ready, k + 1)
                if not (isinstance(k, int) and k == 0 and kk < 2):
                    eng.wait_ge(prod_ready, e - 1)
                for h, cols in halves():
                    last = nc.tensor.matmul(conv[:, unit, cols], wse[:, kk, :], rstk[s][0:RR, cols],
                                            start=True, stop=True)
                last.then_inc(exp_full, 1)

            def add_up(k, s, kk):
                if kk == 0 and not (isinstance(k, int) and k == 0):
                    eng.wait_ge(fin_ready, k)
                if kk == DIRECT:
                    eng.wait_ge(prod_ready, k * TAPS + kk + 1)
                    passes = [(sum_sel[:, kk, :].bitcast(F32), prod[prod_slot(s, kk)])]
                else:
                    if kk in LO_DVE:
                        eng.wait_ge(lo_dve_ready, k * len(LO_DVE) + LO_DVE.index(kk) + 1)
                    else:
                        eng.wait_ge(lo_pool_ready, k * len(LO_POOL) + LO_POOL.index(kk) + 1)
                    slot = SPLIT.index(kk) % RING
                    passes = [(sum_sel[:, kk, :], hi[slot]), (sum_sel[:, kk, :], lo[slot])]
                for n, (sel, src) in enumerate(passes):
                    for h, cols in halves():
                        last = nc.tensor.matmul(att[:, 0, cols], sel, src[:, cols], start=(kk == 0 and n == 0),
                                                stop=(kk == TAPS - 1 and n == len(passes) - 1))
                last.then_inc(sum_done, 1)

            def involve(k, s, first=False, last=False):
                for kk in range(TAPS):
                    expand(k, s, kk)
                    if kk >= LAG:
                        add_up(k, s, kk - LAG)
                    elif not first:
                        add_up(k - 1, 1 - s, TAPS + kk - LAG)
                    m = 2 if first else 3 * k + 2
                    if kk == LAG - 1 and not last:
                        project(k + 1, 1 - s, m, wi[:, :], 128)
                    if kk == LAG + 1 and not last:
                        project(k + 1, 1 - s, m + 1, wr[:, :], AR)
                    if kk == LAG + 3 and not first:
                        turn_back(k - 1, m if last else m + 2)

            eng.wait_ge(wse_ready, 1)
            project(0, 0, 0, wi[:, :], 128)
            project(0, 0, 1, wr[:, :], AR)
            involve(0, 0, first=True)
            eng.wait_ge(misc_free, 4)
            eng.wait_ge(mv_ready, 2 * NP)
            nc.tensor.matmul(att[:, 1, 0:2 * GP], pair_avg[:, :], mv[:, GP:NP, :], start=True, stop=True)\
                .then_inc(misc_full, 1)
            with eng.Fori(0, GP - 1) as i:
                involve(2 * i + 1, 1)
                involve(2 * i + 2, 0)
            involve(NP - 1, 1, last=True)
            for kk in range(TAPS - LAG, TAPS):
                add_up(NP - 1, 1, kk)
            turn_back(NP - 1, 3 * NP)

        @block.scalar
        def _(eng):
            eng.dma_start(ident[:, :], A["c_ident"]).then_inc(turn_consts_in, 16)
            eng.dma_start(pair_avg[:, :], A["c_pair"]).then_inc(turn_consts_in, 16)
            for dst, src in CONSTS:
                eng.dma_start(dst, src).then_inc(consts_in, 16)
            eng.wait_ge(setup, 2)
            nc.scalar.activation(sp[:, 1:2], sp[:, 0:1], ACT.Exp, scale=-1.0).then_inc(setup_act, 1)
            eng.wait_ge(setup_act, 1)
            nc.scalar.activation(sp[:, 2:3], sp[:, 1:2], ACT.Ln, bias=one[:, 0:1]).then_inc(setup_act, 1)

            def turned(k):
                use = Use(-1, ("turn", k))
                eng.wait_ge(att_full, use.full)
                nc.scalar.activation(xin[:, k, :].rearrange("c (p t) -> c p t", t=T),
                                     att[:, use.unit, :].rearrange("c (t p) -> c p t", t=T), ACT.Copy)\
                    .then_inc(att_free[use.unit], 1)

            def normalise(c):
                eng.wait_ge(nmr_ready, c + 1)
                for k in range(c * CH, (c + 1) * CH):
                    nc.scalar.activation(x[:, k, :], xin[:, k, :], ACT.Identity, bias=nmr[:, k:k + 1],
                                         scale=rstd[:, k:k + 1]).then_inc(x_ready, 1)

            def exponentials(p, a):
                use = Use(p, ("scores",))
                eng.wait_ge(negmax_ready, a + 1)
                nc.scalar.activation(attn, att[0:AR, use.unit, :], ACT.Exp, bias=soft[:, 1:2],
                                     accum_out=soft[:, 2:3]).then_inc(att_free[use.unit], 1)

            def route_exp(a):
                eng.wait_ge(shifted_ready, a + 1)
                nc.scalar.activation(rt[:, 3, :, :], rt[:, 2, :, :], ACT.Exp, scale=1.0 / TEMP).then_inc(rexp_ready, 1)

            def factor(p, use, q):
                eng.wait_ge(att_full, use.full)
                if not (isinstance(q, int) and q == 0):
                    eng.wait_ge(xlo_ready, q)
                nc.scalar.activation(xm[:, :], att[:, use.unit, :], ACT.Identity, bias=one[:, 0:1],
                                     scale=gain[:, 0:1]).then_inc(att_free[use.unit], 1)

            def split_hi(q, s):
                eng.wait_ge(comb_step, K * (q + 1))
                for n in range(2):
                    p = slice(64 * n, 64 * n + 64)
                    nc.scalar.activation(whi[p, s, :, 64 * n:64 * n + 64], comb[p, :, :], ACT.Copy).then_inc(whi_ready, 1)
                eng.wait_ge(xm_ready, q + 1)
                nc.scalar.activation(inner(xhi, s), img(xm[:, :]), ACT.Copy).then_inc(xhi_ready, 1)

            def empty_conv(q, s, row, a):
                eng.wait_ge(conv_full, q + 1)
                eng.wait_ge(bias_ready, a + 1)
                nc.scalar.activation(x[:, row, :], conv[:, s, :], ACT.Identity, bias=bias[:, bass.ds(row, 1)])\
                    .then_inc(x_ready, 1)

            def phase(p, g, attend):
                for j in range(GP):
                    q = p * GP + j
                    if j < GP - 1 or attend:
                        factor(p, Use(p, ("map", (j + 1) % GP)), q + 1)
                        split_hi(q + 1, (j + 1) % 2)
                    if attend and j == 0:
                        exponentials(p, p + 1)
                    if attend and j == 6:
                        route_exp(p + 1)
                    empty_conv(q, j % 2, g * GP + j, p)

            for k in range(CH):
                turned(k)
            normalise(0)
            for k in range(CH, GP):
                turned(k)
            normalise(1)
            exponentials(-1, 0)
            for k in range(GP, GP + CH):
                turned(k)
            normalise(2)
            for k in range(GP + CH, NP):
                turned(k)
            route_exp(0)
            eng.wait_ge(setup_done, 1)
            eng.wait_ge(pads_in, 4)
            factor(-1, Use(-1, ("map", 0)), 0)
            split_hi(0, 0)
            normalise(3)
            with eng.Fori(0, PHASES - 1) as p:
                g = eng.snap(p % 2)
                phase(p, g, True)
            phase(PHASES - 1, (PHASES - 1) % 2, False)

            eng.wait_ge(nmr_ready, 5)
            eng.wait_ge(pads_zeroed, 4)

            def normalise2(k, s):
                nc.scalar.activation(xn[s], xin[:, k, :], ACT.Identity, bias=nmr[:, bass.ds(k, 1)],
                                     scale=rstd[:, bass.ds(k, 1)]).then_inc(xn_ready, 1)

            def empty_xi(s, m):
                eng.wait_ge(misc_full, m + 1)
                nc.scalar.activation(xip[s][:, 1:H + 1, 1:W + 1], img(att[:, 1, :]), ACT.Identity, bias=bi_s[:, 0:1])\
                    .then_inc(misc_free, 1)

            def empty_r(k, s, m):
                eng.wait_ge(misc_full, m + 1)
                if not (isinstance(k, int) and k == 0):
                    eng.wait_ge(rstk_ready, k)
                nc.scalar.activation(r96, att[0:AR, 1, :], ACT.Relu, bias=rsc[:, 3:4], scale=rsc[:, 1:2])\
                    .then_inc(misc_free, 1)
                eng.wait_ge(misc_free, m + 1)
                nc.scalar.activation(rstk[s][0:AR, :], r96, ACT.Copy).then_inc(rhi_ready, 1)

            def split_prod(k, s, kk, first):
                n = SPLIT.index(kk)
                eng.wait_ge(prod_ready, k * TAPS + kk + 1)
                if not (first and n < RING):
                    eng.wait_ge(sum_done, (k if n >= RING else k - 1) * TAPS + SPLIT[n - RING] + 1)
                nc.scalar.activation(hi[n % RING], prod[prod_slot(s, kk)], ACT.Copy).then_inc(hi_ready, 1)

            def empty_pix(k, s, m):
                eng.wait_ge(misc_full, m + 1)
                if not (isinstance(k, int) and k < 2):
                    eng.wait_ge(stored[s], (k - s) * 16)
                nc.scalar.activation(pix[s], att[:, 1, :].rearrange("p (t c) -> p t c", t=T), ACT.Copy)\
                    .then_inc(misc_free, 1)

            def involve(k, s, first=False, last=False):
                m = 2 if first else 3 * k + 2
                if not last:
                    normalise2(k + 1, 1 - s)
                for kk in range(TAPS):
                    if kk != DIRECT:
                        split_prod(k, s, kk, first)
                    if kk == 4 and not last:
                        empty_xi(1 - s, m)
                    if kk == 6 and not last:
                        empty_r(k + 1, 1 - s, m + 1)
                    if kk == 8 and not first:
                        empty_pix(k - 1, 1 - s, m if last else m + 2)

            normalise2(0, 0)
            empty_xi(0, 0)
            empty_r(0, 0, 1)
            involve(0, 0, first=True)
            involve(1, 1)
            involve(2, 0)
            eng.wait_ge(nmr_ready, 6)
            with eng.Fori(1, GP - 1) as i:
                involve(2 * i + 1, 1)
                involve(2 * i + 2, 0)
            involve(NP - 1, 1, last=True)
            empty_pix(NP - 1, 1, 3 * NP)

        @block.vector
        def _(eng):
            v = nc.vector
            st = Steps(eng, setup)

            for t in (wi, wr, wq8):
                v.memset(t[:, :], 0.0).then_inc(zeroed, 1)
            eng.wait_ge(zeroed, ZEROS)
            st.start(0)
            eng.wait_ge(consts_in, CONSTS_IN)
            st.then(v.memset(one[:, :], 1.0))
            st.then(v.scalar_tensor_tensor(sp[:, 0:1], alpha[:, :], -1.0, alpha[:, :], ALU.mult, ALU.max))
            st.then(v.tensor_scalar(rsc[:, 0:1], rpar[:, 4:5], BN_EPS, None, ALU.add))
            assert st.n == POW_STEP
            st.then(v.tensor_tensor(tmp32[:, 0:2, 0, :], wk_s[:, :].rearrange("p (n d) -> p n d", n=HEADS),
                                    q_s[:, :].rearrange("p (n d) -> p n d", n=HEADS), ALU.mult))
            st.then(v.tensor_reduce(wq[:, :], tmp32[:, 0:2, 0, :], AX.X, ALU.add))
            for part in range(PARTS):
                for n in range(2):
                    p = slice(64 * n, 64 * n + 64)
                    dst = wq8[p, :].rearrange("p (i r) -> p i r", r=AR + 4)[:, :, 32 * part + 2 * n:32 * part + 2 * n + 2]
                    st.then(v.tensor_scalar(dst, wq[p, :].unsqueeze(1).to_broadcast([64, GP, HEADS]),
                                            DH ** -0.5, None, ALU.mult))
            st.then(v.tensor_tensor(
                tmp32[:, :, :, :],
                wv_s[:, :].rearrange("p (n d) -> p n d", n=HEADS).unsqueeze(2).to_broadcast([128, HEADS, K, DH]),
                wm_s[:, :].rearrange("p (n d k) -> p n k d", n=HEADS, d=DH), ALU.mult))
            st.then(v.tensor_reduce(gate[:, :, :], tmp32[:, :, :, :], AX.X, ALU.add))
            eng.wait_ge(setup_pool, 2)
            st.then(v.tensor_tensor(rsc[:, 1:2], rsc[:, 2:3], rpar[:, 1:2], ALU.mult))
            st.then(v.tensor_tensor(rsc[:, 2:3], rpar[:, 0:1], rpar[:, 3:4], ALU.subtract))
            st.then(v.scalar_tensor_tensor(rsc[:, 3:4], rsc[:, 2:3], rsc[:, 1:2], rpar[:, 2:3], ALU.mult, ALU.add))
            eng.wait_ge(setup_act, 2)
            st.then(v.tensor_scalar(sp[:, 3:4], alpha[:, :], 0.0, sp[:, 2:3], ALU.max, ALU.add))
            st.then(v.tensor_scalar(gain[:, :], sp[:, 3:4], float(S) / HEADS, None, ALU.mult))
            v.memset(allowed[:, :, :, :], 1.0).then_inc(setup_done, 1)

            gn = Steps(eng, gn_step)

            def group_norm(src, lo_k, hi_k, full, freed):
                n = hi_k - lo_k
                avg = src.rearrange("p (k s) -> p k s", s=2)
                rows = mv[:, lo_k:hi_k, :]
                eng.wait_ge(full[0], full[1])
                gn.then(v.tensor_scalar(negmean[:, lo_k:hi_k], avg[:, :, 0], -1.0, None, ALU.mult))
                v.tensor_scalar(gnt[:, 1, 0:n], avg[:, :, 1], GN_EPS, None, ALU.add).then_inc(freed[0], 1)
                eng.wait_ge(freed[0], freed[1])
                gn.then(v.tensor_tensor(gnt[:, 2, 0:n], rows[:, :, 0], negmean[:, lo_k:hi_k], ALU.add))
                gn.then(v.tensor_tensor(gnt[:, 3, 0:n], gnt[:, 2, 0:n], gnt[:, 2, 0:n], ALU.mult))
                v.tensor_tensor(variance[:, lo_k:hi_k], gnt[:, 3, 0:n], gnt[:, 1, 0:n], ALU.add)\
                    .then_inc(variance_ready, 1)

            def softmax(p, a, g):
                use = Use(p, ("scores",))
                so = Steps(eng, soft_step)
                so.start(SOFT_STEPS * a)
                eng.wait_ge(att_full, use.full)
                so.then(v.tensor_reduce(soft[:, 0:1], att[0:AR, use.unit, :], AX.X, ALU.max))
                v.tensor_scalar(soft[:, 1:2], soft[:, 0:1], -1.0, None, ALU.mult).then_inc(negmax_ready, 1)
                eng.wait_ge(att_free[use.unit], use.freed)
                so.then(v.reciprocal(soft[:, 3:4], soft[:, 2:3]))
                so.then(v.tensor_scalar(attn, attn, soft[:, 3:4], None, ALU.mult))
                so.then(v.tensor_copy(parts[:, g, :], attn))
                so.then(v.tensor_tensor(attn, attn, parts[:, g, :], ALU.subtract))
                so.then(v.tensor_copy(parts[32:64, g, :], attn[32:64, :]))
                so.then(v.tensor_copy(parts[64:AR, g, :], attn[64:AR, :]))
                assert so.n == SOFT_STEPS
                v.tensor_tensor(parts[64:AR, g, :], attn[64:AR, :], parts[64:AR, g, :], ALU.subtract)\
                    .then_inc(parts_ready, 1)

            def pool(p, a, g, i, n):
                use = Use(p, ("spread", i, n))
                if i == 0 and n == 0:
                    eng.wait_ge(parts_ready, a + 1)
                else:
                    before = Use(p, ("spread", i - 1 + n, 1 - n))
                    eng.wait_ge(att_free[before.unit], before.freed)
                eng.wait_ge(att_full, use.full)
                v.scalar_tensor_tensor(work[:, :], att[:, use.unit, :], 1.0, x[:, g * GP + i, :], ALU.mult, ALU.mult,
                                       accum_out=pooled[:, i, n:n + 1]).then_inc(att_free[use.unit], 1)

            def bc(ap, axis, shape):
                return ap.unsqueeze(axis).to_broadcast(shape)

            def route(p, a, g):
                sh = [128, GP, K]
                r = Steps(eng, route_step)
                r.start(ROUTE_STEPS * a)
                for n in range(HEADS):
                    use = Use(p, ("spread", GP - 1, n))
                    eng.wait_ge(att_free[use.unit], use.freed)
                for n in range(HEADS):
                    r.then(v.tensor_tensor(zt[:, n, :, :], bc(pooled[:, :, n], 2, sh), bc(gate[:, n, :], 1, sh), ALU.mult))
                v.tensor_tensor(zt[:, 0, :, :], zt[:, 0, :, :], zt[:, 1, :, :], ALU.add).then_inc(gated_ready, 1)
                use = Use(p, ("logits",))
                eng.wait_ge(att_full, use.full)
                ok = allowed[:, g, :, :]
                v.tensor_tensor(rt[:, 0, :, :], att[:, use.unit, 0:GP * K].rearrange("p (i k) -> p i k", k=K), ok,
                                ALU.mult).then_inc(att_free[use.unit], 1)
                eng.wait_ge(att_free[use.unit], use.freed)
                r.then(v.tensor_scalar(rt[:, 1, :, :], ok, -1.0, 1e9, ALU.add, ALU.mult))
                r.then(v.tensor_tensor(rt[:, 0, :, :], rt[:, 0, :, :], rt[:, 1, :, :], ALU.add))
                r.then(v.tensor_reduce(rs[:, 0, :], rt[:, 0, :, :], AX.X, ALU.max))
                v.tensor_tensor(rt[:, 2, :, :], rt[:, 0, :, :], bc(rs[:, 0, :], 2, sh), ALU.subtract)\
                    .then_inc(shifted_ready, 1)
                eng.wait_ge(rexp_ready, a + 1)
                r.then(v.tensor_reduce(rs[:, 1, :], rt[:, 3, :, :], AX.X, ALU.add))
                r.then(v.reciprocal(rs[:, 2, :], rs[:, 1, :]))
                w = rt[:, 4, :, :]
                r.then(v.tensor_tensor(w, rt[:, 3, :, :], bc(rs[:, 2, :], 2, sh), ALU.mult))
                full = [128, GP, K, K]
                wj, we = bc(w, 2, full), bc(w, 3, full)
                r.then(v.tensor_tensor(cmp[:, 0, :, :, :], wj, we, ALU.is_gt))
                r.then(v.tensor_tensor(cmp[:, 1, :, :, :], wj, we, ALU.is_equal))
                r.then(v.tensor_tensor(cmp[:, 2, :, :, :], cmp[:, 1, :, :, :], bc(earlier[:, :, :], 1, full), ALU.mult))
                r.then(v.tensor_tensor(cmp[:, 1, :, :, :], cmp[:, 2, :, :, :], cmp[:, 0, :, :, :], ALU.add))
                r.then(v.tensor_reduce(rt[:, 5, :, :], cmp[:, 1, :, :, :], AX.X, ALU.add))
                r.then(v.tensor_scalar(rt[:, 6, :, :], rt[:, 5, :, :], 1.5, None, ALU.is_lt))
                r.then(v.tensor_tensor(rt[:, 7, :, :], w, rt[:, 6, :, :], ALU.mult))
                r.then(v.tensor_reduce(rs[:, 3, :], rt[:, 7, :, :], AX.X, ALU.add))
                r.then(v.tensor_scalar(rs[:, 4, :], rs[:, 3, :], 1e-9, None, ALU.add))
                r.then(v.reciprocal(rs[:, 5, :], rs[:, 4, :]))
                r.then(v.tensor_tensor(wsel[:, :, :], rt[:, 7, :, :], bc(rs[:, 5, :], 2, sh), ALU.mult))
                r.then(v.tensor_scalar(rt[:, 8, :, :], rt[:, 5, :, :], 0.5, None, ALU.is_lt))
                some = allowed[:, g, :, 0:K - 1]
                r.then(v.tensor_tensor(rt[:, 9, :, 0:K - 1], some, rt[:, 8, :, 0:K - 1], ALU.subtract))
                r.then(v.tensor_scalar(some, rt[:, 9, :, 0:K - 1], 0.0, 1.0, ALU.max, ALU.min))
                r.then(v.tensor_tensor(rt[:, 10, :, :], wsel[:, :, :], bc(be_s[:, :], 1, sh), ALU.mult))
                assert r.n == ROUTE_STEPS
                v.tensor_reduce(bias[:, bass.ds(g * GP, GP)] if not isinstance(g, int) else bias[:, g * GP:(g + 1) * GP],
                                rt[:, 10, :, :], AX.X, ALU.add).then_inc(bias_ready, 1)

            def modulate(p, g, i, q):
                use = Use(p, ("map", i))
                eng.wait_ge(att_free[use.unit], use.freed)
                v.tensor_tensor(xm[:, :], xm[:, :], x[:, g * GP + i, :], ALU.mult).then_inc(xm_ready, 1)

            def combine(i, q):
                if not (isinstance(q, int) and q == 0):
                    eng.wait_ge(wlo_ready, 2 * q)
                cflat = comb[:, :, :].rearrange("p a b -> p (a b)")
                v.tensor_scalar(cflat, experts[:, 0, :], wsel[:, i, 0:1], None, ALU.mult).then_inc(comb_step, 1)
                for e in range(1, K):
                    eng.wait_ge(comb_step, K * q + e)
                    v.scalar_tensor_tensor(cflat, experts[:, e, :], wsel[:, i, e:e + 1], cflat, ALU.mult, ALU.add)\
                        .then_inc(comb_step, 1)

            def channel_stats(k):
                for n in range(2):
                    gn.then(v.bn_stats(stats[:, k, n, :], xin[:, k, n * HW:(n + 1) * HW]))
                v.bn_aggr(mv[:, k, :], stats[:, k, :, :]).then_inc(mv_ready, 1)

            def turned_stats(k):
                use = Use(-1, ("turn", k))
                eng.wait_ge(att_free[use.unit], use.freed)
                channel_stats(k)

            def chunk_norm(c):
                use = Use(-1, ("gn", c))
                group_norm(att[:, use.unit, 0:2 * CH], CH * c, CH * c + CH, (att_full, use.full),
                           (att_free[use.unit], use.freed))

            def residual(n):
                k = RESIDUAL[n]
                eng.wait_ge(x_ready, NP + GP * (PHASES - 1) + (k - GP + 1 if k >= GP else 0))
                v.tensor_tensor(xin[:, k, :], xin[:, k, :], x[:, k, :], ALU.add).then_inc(x1_step, 1)
                eng.wait_ge(x1_step, n + 1)
                channel_stats(k)

            gn.start(0)
            for c in range(2):
                for k in range(CH * c, CH * c + CH):
                    turned_stats(k)
                chunk_norm(c)
            softmax(-1, 0, 0)
            for i in range(GP):
                for n in range(HEADS):
                    pool(-1, 0, 0, i, n)
                turned_stats(GP + i)
                if i == CH - 1:
                    chunk_norm(2)
            route(-1, 0, 0)
            combine(0, 0)
            modulate(-1, 0, 0, 0)
            chunk_norm(3)

            def phase(p, g, ng, attend):
                for j in range(GP):
                    q = p * GP + j
                    if j < GP - 1:
                        combine(j + 1, q + 1)
                        modulate(p, g, j + 1, q + 1)
                    elif attend:
                        combine(0, q + 1)
                        modulate(p, ng, 0, q + 1)
                    if attend:
                        if j == 0:
                            softmax(p, p + 1, ng)
                        for key, _ in slot_uses(j):
                            if key[0] == "spread":
                                pool(p, p + 1, ng, key[1], key[2])
                        if j == 6:
                            route(p, p + 1, ng)
                    else:
                        residual(RESIDUAL.index(j))
                        if j >= 2:
                            residual(RESIDUAL.index(j) + 1)

            with eng.Fori(0, PHASES - 1) as p:
                g = eng.snap(p % 2)
                ng = eng.snap((p + 1) % 2)
                phase(p, g, ng, True)
            phase(PHASES - 1, (PHASES - 1) % 2, None, False)

            late = Steps(eng, late_setup)
            eng.wait_ge(late_consts_in, 16 * len(LATE_CONSTS))
            late.then(v.tensor_copy(sum_sel[:, :, :].rearrange("p a b -> p (a b)"), st_sum))
            late.then(v.tensor_copy(
                st_exp.rearrange("p (g j t) -> p g j t", g=G16, j=C // G16),
                st_ws.rearrange("p (g t) -> p g t", g=G16).unsqueeze(2).to_broadcast([RR, G16, C // G16, TAPS])))
            for n in range(2):
                late.then(v.tensor_scalar(st_bd[:, :, 64 * n:64 * n + 64], st_exp.rearrange("p (t c) -> p t c", t=TAPS),
                                        masks[:, n:n + 1], None, ALU.mult))
            hi_of = wse[:, :, :].rearrange("p a b -> p (a b)")
            bd = st_bd.rearrange("p t c -> p (t c)")
            late.then(v.tensor_copy(hi_of, bd))
            late.then(v.tensor_tensor(bd, bd, hi_of.bitcast(F32), ALU.subtract))
            late.then(v.tensor_scalar(bd, bd, masks[:, 2:3], None, ALU.mult))
            v.scalar_tensor_tensor(hi_of, hi_of.bitcast(F32), masks[:, 3:4], bd, ALU.mult, ALU.add).then_inc(wse_ready, 1)
            use = Use(PHASES - 1, ("gn", 4))
            group_norm(att[:, use.unit, 0:2 * GP], 0, GP, (att_full, use.full), (att_free[use.unit], use.freed))
            for n in range(2):
                v.memset(xip[n], 0.0).then_inc(pads_zeroed, 1)
                v.memset(rstk[n][AR:RR, :].bitcast(F32), 1.0).then_inc(pads_zeroed, 1)
            residual(NP - 2)
            residual(NP - 1)

            def product(k, s, kk, first, second):
                e = k * TAPS + kk
                unit = (s * TAPS + kk) % 2
                kh, kw = divmod(kk, 3)
                eng.wait_ge(exp_full, e + 1)
                if kk == 0:
                    eng.wait_ge(misc_free, 1 if first else 3 if second else 3 * k)
                old = (kk - PRODS) % TAPS
                before = k if kk >= PRODS else k - 1
                if not (first and kk < PRODS):
                    if old == DIRECT:
                        eng.wait_ge(sum_done, before * TAPS + old + 1)
                    elif old in LO_POOL:
                        eng.wait_ge(lo_pool_ready, before * len(LO_POOL) + LO_POOL.index(old) + 1)
                    else:
                        eng.wait_ge(lo_dve_ready, before * len(LO_DVE) + LO_DVE.index(old) + 1)
                v.tensor_tensor(img(prod[prod_slot(s, kk)]), img(conv[:, unit, :]), xip[s][:, kh:kh + H, kw:kw + W], ALU.mult)\
                    .then_inc(prod_ready, 1)

            def split_lo(k, s, kk):
                slot = SPLIT.index(kk) % RING
                eng.wait_ge(hi_ready, k * len(SPLIT) + SPLIT.index(kk) + 1)
                v.tensor_tensor(lo[slot], prod[prod_slot(s, kk)], hi[slot].bitcast(F32), ALU.subtract).then_inc(lo_dve_ready, 1)

            def finish(k, m):
                eng.wait_ge(sum_done, TAPS * (k + 1))
                if m is not None:
                    eng.wait_ge(misc_full, m)
                v.tensor_tensor(fin, att[:, 0, :], xin[:, k, :], ALU.add).then_inc(fin_ready, 1)

            def involve(k, s, first=False, second=False):
                for kk in range(TAPS):
                    product(k, s, kk, first, second)
                    if kk - 2 in LO_DVE:
                        split_lo(k, s, kk - 2)
                    if kk == LAG - 1 and not first:
                        finish(k - 1, None if second else 3 * k + 2)

            involve(0, 0, first=True)
            group_norm(att[:, 1, 0:2 * GP], GP, NP, (misc_full, 5), (misc_free, 5))
            involve(1, 1, second=True)
            involve(2, 0)
            with eng.Fori(1, GP - 1) as i:
                involve(2 * i + 1, 1)
                involve(2 * i + 2, 0)
            involve(NP - 1, 1)
            finish(NP - 1, 3 * NP)

        @block.gpsimd
        def _(eng):
            v = nc.gpsimd
            v.memset(mhalf[:, :], -0.5).then_inc(setup_pool, 1)
            for t in (xhi, xlo, whi, wlo):
                v.memset(t[:, :, :, :].bitcast(F32), 0.0).then_inc(pads_in, 1)
            eng.wait_ge(setup, POW_STEP)
            eng.wait_ge(setup_pool, 1)
            v.tensor_tensor(rsc[:, 2:3], rsc[:, 0:1], mhalf[0:AR, 0:1], ALU.pow).then_inc(setup_pool, 1)
            eng.wait_ge(pads_in, 4)

            def inverse_root(c, lo_k, hi_k):
                n = hi_k - lo_k
                eng.wait_ge(variance_ready, c + 1)
                v.tensor_tensor(rstd[:, lo_k:hi_k], variance[:, lo_k:hi_k], mhalf[:, 0:n], ALU.pow)\
                    .then_inc(inverse_ready, 1)
                eng.wait_ge(inverse_ready, c + 1)
                v.tensor_tensor(nmr[:, lo_k:hi_k], negmean[:, lo_k:hi_k], rstd[:, lo_k:hi_k], ALU.mult)\
                    .then_inc(nmr_ready, 1)

            def split_lo(q, s):
                eng.wait_ge(whi_ready, 2 * q + 2)
                if isinstance(q, int) and q == 0:
                    eng.wait_ge(nmr_ready, 3)
                else:
                    eng.wait_ge(xlo_ready, q)
                for n in range(2):
                    p = slice(64 * n, 64 * n + 64)
                    v.tensor_tensor(wlo[p, s, :, 64 * n:64 * n + 64], comb[p, :, :],
                                    whi[p, s, :, 64 * n:64 * n + 64].bitcast(F32), ALU.subtract).then_inc(wlo_ready, 1)
                    eng.wait_ge(wlo_ready, 2 * q + n + 1)
                eng.wait_ge(xhi_ready, q + 1)
                v.tensor_tensor(inner(xlo, s), img(xm[:, :]), inner(xhi, s).bitcast(F32), ALU.subtract)\
                    .then_inc(xlo_ready, 1)

            for c in range(3):
                inverse_root(c, CH * c, CH * c + CH)
            split_lo(0, 0)
            eng.wait_ge(xlo_ready, 1)
            inverse_root(3, 3 * CH, NP)
            with eng.Fori(0, PHASES - 1) as p:
                for j in range(GP):
                    split_lo(p * GP + j + 1, (j + 1) % 2)
            for j in range(GP - 1):
                split_lo((PHASES - 1) * GP + j + 1, (j + 1) % 2)

            eng.wait_ge(xlo_ready, PHASES * GP)
            inverse_root(4, 0, GP)

            def r_lo(k, s):
                if isinstance(k, int) and k == 0:
                    eng.wait_ge(nmr_ready, 5)
                else:
                    eng.wait_ge(lo_pool_ready, (k - 1) * len(LO_POOL) + LO_POOL.index(R_AFTER) + 1)
                eng.wait_ge(rhi_ready, k + 1)
                v.tensor_tensor(rstk[s][32:64, :], r96[32:64, :], rstk[s][32:64, :].bitcast(F32), ALU.subtract)\
                    .then_inc(rstk_ready, 1)
                eng.wait_ge(rstk_ready, k + 1)

            def involve(k, s, last=False):
                for kk in range(TAPS):
                    if kk in LO_POOL:
                        slot = SPLIT.index(kk) % RING
                        eng.wait_ge(hi_ready, k * len(SPLIT) + SPLIT.index(kk) + 1)
                        v.tensor_tensor(lo[slot], prod[prod_slot(s, kk)], hi[slot].bitcast(F32), ALU.subtract)\
                            .then_inc(lo_pool_ready, 1)
                    if kk == R_AFTER and not last:
                        r_lo(k + 1, 1 - s)

            r_lo(0, 0)
            involve(0, 0)
            eng.wait_ge(rstk_ready, 2)
            inverse_root(5, GP, NP)
            involve(1, 1)
            with eng.Fori(1, GP - 1) as i:
                involve(2 * i, 0)
                involve(2 * i + 1, 1)
            involve(NP - 2, 0)
            involve(NP - 1, 1, last=True)


def constants():
    rows = np.arange(AR)
    spread = np.zeros((AR, GP, 3, 128), np.float32)
    for i in range(GP):
        for image in range(2):
            for head in range(HEADS):
                hit = rows % 32 == 4 * i + 2 * image + head
                spread[hit, i, head, 64 * image:64 * image + 64] = 1
                spread[hit, i, 2, 64 * image:64 * image + 64] = 1
    ch = np.arange(128)
    total = np.zeros((128, TAPS, 128), np.float32)
    for t in range(TAPS):
        for c in range(C):
            for image in range(2):
                total[64 * image + c, t, 64 * image + (t * C + c) // TAPS] = 1
    row = np.arange(RR)
    low = ((row >= 64) & (row < 96)) | (row == 97)
    masks = np.stack([(row % 32 < CR) | (row >= AR), (row % 32 >= CR) | (row >= AR), low, ~low], 1).astype(np.float32)
    return {
        "c_spread": spread.reshape(AR, -1).astype(np.uint16) * np.uint16(BF16_ONE),
        "c_ident": np.eye(128, dtype=np.float32),
        "c_pair": np.where(ch[:, None] // 2 == ch // 2, 0.5, 0).astype(np.float32),
        "c_same": (ch[:, None] // 64 == ch // 64).astype(np.float32),
        "c_sum": total.reshape(128, -1),
        "c_masks": masks,
        "c_earlier": np.tril(np.ones((K, K), np.float32), -1).reshape(1, -1)[0],
    }


def kernel(**inputs):
    import concourse.bacc as bacc
    from concourse.bass_utils import run_bass_kernel_spmd

    a = {n: np.ascontiguousarray(v) for n, v in inputs.items()}
    arrays = {
        "x": a["x"].reshape(B, S, C),
        "q": a["L0_conv_q"].reshape(D), "Wk": a["L0_conv_Wk"], "Wv": a["L0_conv_Wv"],
        "Wmlp": a["L0_conv_Wmlp"].reshape(D * K), "alpha": a["L0_conv_alpha"].reshape(1),
        "We": a["L0_conv_We"].reshape(K * TAPS, C, C), "be": np.ascontiguousarray(a["L0_conv_be"].T),
        "rpar": np.ascontiguousarray(np.tile(np.stack(
            [a["L1_conv_" + n] for n in ("br", "gamma", "beta", "mean", "var")], 1), (2 * PARTS, 1))),
        "Wr": a["L1_conv_Wr"], "Ws": a["L1_conv_Ws"], "bs": a["L1_conv_bs"], "Wi": a["L1_conv_Wi"],
        "bi": a["L1_conv_bi"].reshape(C, 1),
        **constants(),
    }
    nc = bacc.Bacc("TRN2", target_bir_lowering=False, num_devices=1)
    A = {n: nc.dram_tensor("in_" + n, v.shape, mybir.dt.from_np(v.dtype), kind="ExternalInput").ap()
         for n, v in arrays.items()}
    out = nc.dram_tensor("out", (B, S, C), F32, kind="ExternalOutput").ap()
    build(nc, A, out)
    r = run_bass_kernel_spmd(nc, [{"in_" + n: v for n, v in arrays.items()}], core_ids=[0])
    return r.results[0]["out"].reshape(B, H, W, C)
```

```python
from contextlib import ExitStack

import numpy as np

import concourse.bass as bass
from concourse import mybir

F32 = mybir.dt.float32
F32R = mybir.dt.float32r
BF16 = mybir.dt.bfloat16
ALU = mybir.AluOpType
ACT = mybir.ActivationFunctionType
AX = mybir.AxisListType

B, H, W, C = 32, 32, 32, 64
S = H * W
NP = B // 2
GP = NP // 2
HW = S // 2
PW = W + 2
PS = PW * PW
K = 4
HEADS, DH = 2, 16
D = HEADS * DH
STEPS = 3
PHASES = 2 * STEPS
TEMP = 1.5
TAPS = 9
CR = 16
G16 = 16
GN_EPS = 1e-5
BN_EPS = 1e-3
PARTS = 3
AR = PARTS * 4 * GP
RR = 98
T = S // 128

CH = 4
PROLOGUE_USES = (
    [("turn", k) for k in range(CH + 2)] + [("gn", 0)] + [("turn", k) for k in range(CH + 2, GP)]
    + [("gn", 1), ("scores",), ("gn", 2)] + [("spread", i, n) for i in range(CH + 2) for n in range(HEADS)] + [("gn", 3)]
    + [("spread", i, n) for i in range(CH + 2, GP) for n in range(HEADS)] + [("logits",), ("map", 0)]
)


POOLS = (1, 3, 3, 2, 3, 2, 2, 0)
POOL_TAPS = {0: (), 1: (17,), 2: (5, 11), 3: (4, 9, 14)}
LOGITS_TAP = 6
assert sum(POOLS) == GP * HEADS


def slot_uses(j, last=False):
    if last:
        return [(("map", j + 1), 0)] if j < GP - 1 else [(("gn", 4), 2 * TAPS - 1)]
    uses = [(("map", 1), -1), (("scores",), -1)] if j == 0 else [(("map", (j + 1) % GP), 0)]
    first = sum(POOLS[:j])
    uses += [(("spread", (first + m) // HEADS, (first + m) % HEADS), POOL_TAPS[POOLS[j]][m]) for m in range(POOLS[j])]
    if j == GP - 1:
        uses += [(("logits",), LOGITS_TAP)]
    return uses


PHASE_USES = [key for j in range(GP) for key, _ in slot_uses(j)]
LAST_USES = [key for j in range(GP) for key, _ in slot_uses(j, True)]
assert len(PHASE_USES) % 2 == 0
RESIDUAL = [k for j in range(GP) for k in ([j] if j < 2 else [j, GP + j - 2])] + [NP - 2, NP - 1]


class Use:

    def __init__(self, p, key):
        if isinstance(p, int) and p == -1:
            at = PROLOGUE_USES.index(key)
            self.unit, self.before, self.full = at % 2, at // 2, at + 1
        elif isinstance(p, int) and p == PHASES - 1:
            at = len(PROLOGUE_USES) + p * len(PHASE_USES) + LAST_USES.index(key)
            self.unit, self.before, self.full = at % 2, at // 2, at + 1
        else:
            at = len(PROLOGUE_USES) + PHASE_USES.index(key)
            self.unit = at % 2
            self.before = p * (len(PHASE_USES) // 2) + at // 2
            self.full = p * len(PHASE_USES) + at + 1
        self.freed = self.before + 1


class Steps:

    def __init__(self, eng, sem):
        self.eng, self.sem, self.base, self.n = eng, sem, 0, 0

    def start(self, base):
        self.base, self.n = base, 0

    def then(self, instruction):
        self.n += 1
        instruction.then_inc(self.sem, 1)
        self.eng.wait_ge(self.sem, self.base + self.n)


BF16_ONE = 0x3F80
SOFT_STEPS, ROUTE_STEPS, LATE_STEPS = 7, 23, 5
POW_STEP, WQ_STEP = 3, 11
WSEL_STEP = 19
DIRECT = 4
LO_DVE = (1, 3, 6)
LO_POOL = tuple(t for t in range(TAPS) if t != DIRECT and t not in LO_DVE)
SPLIT = tuple(t for t in range(TAPS) if t != DIRECT)
PRODS = 6
RING = 4
T_AT = 8
R_AFTER = 5
LAG = 4
assert 2 * TAPS % PRODS == 0 and len(SPLIT) % RING == 0


def build(nc, A, out):
    ctx = ExitStack()
    with ctx:
        def sb(name, shape, dt=F32):
            return ctx.enter_context(nc.sbuf_tensor(name, shape, dt))

        def sem(name):
            return ctx.enter_context(nc.semaphore(name))

        xin = sb("xin", [128, NP, S])
        x = sb("x", [128, NP, S])
        with ExitStack() as routed_only:
            experts = routed_only.enter_context(nc.sbuf_tensor("experts", [128, K, TAPS * C], F32))
            work = routed_only.enter_context(nc.sbuf_tensor("work", [128, S], F32))
            parts = routed_only.enter_context(nc.sbuf_tensor("parts", [AR, 2, S], BF16))
        attn = work[0:AR, :]
        cmp = work[:, 0:3 * GP * K * K].rearrange("p (a i e j) -> p a i e j", a=3, i=GP, e=K)
        sum_sel = sb("sum_sel", [128, TAPS, 128], F32R)
        wse = sb("wse", [RR, TAPS, 128], F32R)
        rstack = sb("rstack", [128, 2, S], F32R)
        comb = sb("comb", [128, TAPS, C])
        wa = sb("wa", [128, 2, TAPS, 128], F32R)
        wb = sb("wb", [128, 2, TAPS, 128], F32R)
        xa = sb("xa", [128, 2, PW, PW], F32R)
        xb = sb("xb", [128, 2, PW, PW], F32R)
        xm = sb("xm", [128, S])
        main = sb("main", [128, S])
        wk_s, q_s, wv_s = (main[:, n * D:(n + 1) * D] for n in range(3))
        wm_s = main[:, 3 * D:(3 + K) * D]
        tmp32 = main[:, (3 + K) * D:(3 + 2 * K) * D].rearrange("p (n k d) -> p n k d", n=HEADS, k=K)
        spread_sel = sb("spread_sel", [AR, GP * 3, 128], BF16)
        ident = sb("ident", [128, 128])
        pair_avg = sb("pair_avg", [128, 128])
        same_image = sb("same_image", [128, 128])
        wi = sb("wi", [128, 128])
        wr = sb("wr", [128, AR])
        wq8 = sb("wq8", [128, 800])
        wq = sb("wq", [128, HEADS])
        gate = sb("gate", [128, HEADS, K])
        be_s = sb("be_s", [128, K])
        earlier = sb("earlier", [128, K, K])
        alpha = sb("alpha", [128, 1])
        sp = sb("sp", [128, 4])
        gain = sb("gain", [128, 1])
        one = sb("one", [128, 1])
        mhalf = sb("mhalf", [128, 2 * NP])
        masks = sb("masks", [RR, 4])
        rpar = sb("rpar", [AR, 5])
        rsc = sb("rsc", [AR, 4])
        bi_s = sb("bi_s", [128, 1])
        stats = sb("stats", [128, NP, 2, 6])
        mv = sb("mv", [128, NP, 2])
        gnt = sb("gnt", [128, 4, NP])
        negmean = sb("negmean", [128, NP])
        variance = sb("variance", [128, NP])
        rstd = sb("rstd", [128, NP])
        nmr = sb("nmr", [128, NP])
        soft = sb("soft", [AR, 4])
        pooled = sb("pooled", [128, GP, HEADS])
        zt = sb("zt", [128, 2, GP, K])
        rt = sb("rt", [128, 12, GP, K])
        rs = sb("rs", [128, 6, GP])
        wsel = sb("wsel", [128, GP, K])
        allowed = sb("allowed", [128, 2, GP, K])
        bias = sb("bias", [128, NP])

        xpix = [x[:, GP + n, :].rearrange("p (t c) -> p t c", t=T) for n in range(GP)]
        stage = x[:, 0:3, :].rearrange("p a b -> p (a b)")
        st_sum = stage[:, 0:TAPS * 128]
        st_ws = stage[0:RR, 1152:1152 + TAPS * G16]
        st_exp = stage[0:RR, 1296:1296 + TAPS * C]
        st_bd = stage[0:RR, 1872:1872 + TAPS * 128].rearrange("p (t c) -> p t c", t=TAPS)

        conv = ctx.enter_context(nc.psum_tensor("conv", [128, 2, S], F32))
        att = ctx.enter_context(nc.psum_tensor("att", [128, 2, S], F32))

        consts_in = sem("consts_in")
        late_consts_in = sem("late_consts_in")
        late_setup = sem("late_setup")
        late_lo = sem("late_lo")
        wse_ready = sem("wse_ready")
        pix_in = [sem(f"pix_in{n}") for n in range(GP)]
        turn_consts_in = sem("turn_consts_in")
        pads_in = sem("pads_in")
        variance_ready = sem("variance_ready")
        inverse_ready = sem("inverse_ready")
        zeroed = sem("zeroed")
        setup = sem("setup")
        setup_pool = sem("setup_pool")
        setup_act = sem("setup_act")
        setup_done = sem("setup_done")
        att_full = sem("att_full")
        att_free = [sem("att_free0"), sem("att_free1")]
        second_turned = sem("second_turned")
        second_emptied = sem("second_emptied")
        gn_step = sem("gn_step")
        nmr_ready = sem("nmr_ready")
        x_ready = sem("x_ready")
        soft_step = sem("soft_step")
        negmax_ready = sem("negmax_ready")
        exp_ready = sem("exp_ready")
        parts_ready = sem("parts_ready")
        gated_ready = sem("gated_ready")
        route_step = sem("route_step")
        shifted_ready = sem("shifted_ready")
        rexp_ready = sem("rexp_ready")
        bias_ready = sem("bias_ready")
        xm_ready = sem("xm_ready")
        xhi_ready = sem("xhi_ready")
        xlo_ready = sem("xlo_ready")
        comb_step = sem("comb_step")
        main_ready = sem("main_ready")
        whi_ready = sem("whi_ready")
        wlo_ready = sem("wlo_ready")
        conv_full = sem("conv_full")
        x1_step = sem("x1_step")
        mv_ready = sem("mv_ready")
        pads_zeroed = sem("pads_zeroed")
        misc_full = sem("misc_full")
        misc_free = sem("misc_free")
        xn_ready = sem("xn_ready")
        xi_ready = sem("xi_ready")
        r_ready = sem("r_ready")
        rhi_ready = sem("rhi_ready")
        rstk_ready = sem("rstk_ready")
        exp_full = sem("exp_full")
        prod_ready = sem("prod_ready")
        hi_ready = sem("hi_ready")
        lo_dve_ready = sem("lo_dve_ready")
        lo_pool_ready = sem("lo_pool_ready")
        sum_done = sem("sum_done")
        fin_ready = sem("fin_ready")
        stored = [sem("stored0"), sem("stored1")]

        flat = x[:, :, :].rearrange("p a b -> p (a b)")
        prod = [flat[:, n * S:(n + 1) * S] for n in range(PRODS)]
        xn = [flat[:, (6 + n) * S:(7 + n) * S] for n in range(2)]
        r96 = flat[0:AR, 8 * S:9 * S]
        xip = [flat[:, 9 * S + n * PS:9 * S + (n + 1) * PS].rearrange("p (a b) -> p a b", a=PW)
               for n in range(2)]
        fin = flat[:, 12 * S:13 * S]
        pix = [flat[:, (13 + n) * S:(14 + n) * S].rearrange("p (t c) -> p t c", t=T) for n in range(2)]

        def pad_flat(t, n):
            return t[:, n, :, :].rearrange("p a b -> p (a b)")[:, 0:S]

        hi = [pad_flat(t, n) for t in (xa, wa) for n in range(2)]
        lo = [pad_flat(t, n) for t in (xb, wb) for n in range(2)]
        rstk = [rstack[:, n, :] for n in range(2)]

        def prod_slot(s, kk):
            return (s * TAPS + kk) % PRODS

        def img(ap):
            return ap.rearrange("p (a b) -> p a b", a=H)

        def inner(padded, p, s):
            return padded[p, s, 1:H + 1, 1:W + 1]

        own = (slice(0, 64), slice(64, 128))
        other = (own[1], own[0])
        xs, ws = (xa, xb), (wa, wb)

        def halves():
            return ((h, slice(h * HW, (h + 1) * HW)) for h in range(2))

        CONSTS = [
            (spread_sel[:, :, :].rearrange("p a b -> p (a b)").bitcast(mybir.dt.uint16), A["c_spread"]),
            (same_image[:, :], A["c_same"]), (masks[:, :], A["c_masks"]),
            (earlier[:, :, :].rearrange("p a b -> p (a b)"), A["c_earlier"].partition_broadcast(128)),
            (q_s[:, :], A["q"].partition_broadcast(128)),
            (wm_s[:, :], A["Wmlp"].partition_broadcast(128)),
            (alpha[:, :], A["alpha"].partition_broadcast(128)),
            (rpar[:, :], A["rpar"]),
        ]
        for n in range(2):
            p = slice(64 * n, 64 * n + 64)
            CONSTS += [
                (wk_s[p, :], A["Wk"]), (wv_s[p, :], A["Wv"]), (be_s[p, :], A["be"]),
                (experts[p, :, :].rearrange("p k (t c) -> p (k t) c", t=TAPS), A["We"].rearrange("t i o -> i t o")),
                (bi_s[p, :], A["bi"]),
            ]
        LATE_CONSTS = [(st_sum, A["c_sum"]), (st_ws[AR:RR, :], A["bs"].partition_broadcast(2))]
        LATE_CONSTS += [(st_ws[CR * a:CR * a + CR, :], A["Ws"]) for a in range(2 * PARTS)]
        BLOCKS = [(wi[64 * n:64 * n + 64, 64 * n:64 * n + 64], A["Wi"]) for n in range(2)]
        BLOCKS += [(wr[64 * n:64 * n + 64, 32 * a + CR * n:32 * a + CR * n + CR], A["Wr"])
                   for n in range(2) for a in range(PARTS)]
        CONSTS_IN = 16 * (len(CONSTS) + len(BLOCKS))
        ZEROS = 3

        block = ctx.enter_context(nc.Block())

        @block.sync
        def _(eng):
            def load_pair(k, n):
                for m in range(2):
                    eng.dma_start(xpix[n][:, :, 64 * m:64 * m + 64],
                                  A["x"][2 * k + m, :, :].rearrange("(p t) c -> p t c", t=T)).then_inc(pix_in[n], 16)

            for k in range(GP):
                load_pair(k, k)
            for dst, src in CONSTS:
                eng.dma_start(dst, src).then_inc(consts_in, 16)
            eng.wait_ge(zeroed, ZEROS)
            for dst, src in BLOCKS:
                eng.dma_start(dst, src).then_inc(consts_in, 16)
            for n in range(GP):
                eng.wait_ge(att_full, Use(-1, ("turn", n)).full)
                load_pair(GP + n, n)
            eng.wait_ge(x1_step, RESIDUAL.index(2) + 1)
            for dst, src in LATE_CONSTS:
                eng.dma_start(dst, src).then_inc(late_consts_in, 16)

            def store_pair(k, n, uses):
                eng.wait_ge(misc_free, uses)
                for m in range(2):
                    eng.dma_start(out[2 * k + m, :, :].rearrange("(p t) c -> p t c", t=T),
                                  pix[n][:, :, 64 * m:64 * m + 64]).then_inc(stored[n], 16)

            with eng.Fori(0, GP - 1) as i:
                for n in range(2):
                    store_pair(2 * i + n, n, 6 * i + 3 * n + 8)
            for n in range(2):
                store_pair(NP - 2 + n, n, 3 * NP + n)
            for n in range(2):
                eng.wait_ge(stored[n], 2 * 16 * GP)

        @block.tensor
        def _(eng):
            def claim(use):
                if not (isinstance(use.before, int) and use.before == 0):
                    eng.wait_ge(att_free[use.unit], use.before)

            def turn(k):
                if k < GP:
                    use = Use(-1, ("turn", k))
                    claim(use)
                    unit, full = att[:, use.unit, :], att_full
                else:
                    unit, full = conv[:, k % 2, :], second_turned
                    if k >= GP + 2:
                        eng.wait_ge(second_emptied, k - GP - 1)
                eng.wait_ge(pix_in[k % GP], 32 * (k // GP + 1))
                for t in range(T):
                    last = nc.tensor.transpose(unit[:, 128 * t:128 * t + 128], xpix[k % GP][:, t, :], ident[:, :])
                last.then_inc(full, 1)

            def group_average(p, c, lo_k, hi_k, value):
                use = Use(p, ("gn", c))
                claim(use)
                eng.wait_ge(mv_ready, value)
                nc.tensor.matmul(att[:, use.unit, 0:2 * (hi_k - lo_k)], pair_avg[:, :], mv[:, lo_k:hi_k, :],
                                 start=True, stop=True).then_inc(att_full, 1)

            def scores(p, a, g):
                use = Use(p, ("scores",))
                claim(use)
                prologue = isinstance(a, int) and a == 0
                if not prologue:
                    eng.wait_ge(x_ready, NP)
                for i in range(GP):
                    eng.wait_ge(x_ready, i + 1 if prologue else NP + 2 * GP * (p - 1) + 2 * (i + 1))
                    for h, cols in halves():
                        last = nc.tensor.matmul(att[0:AR, use.unit, cols], wq8[:, AR * i:AR * i + AR],
                                                x[:, g * GP + i, cols], start=(i == 0), stop=(i == GP - 1))
                    if prologue and i % 2 == 1 and i < GP - 1:
                        turn(GP + i // 2)
                last.then_inc(att_full, 1)

            def spread(p, a, g, i, n):
                use = Use(p, ("spread", i, n))
                claim(use)
                if i == 0 and n == 0:
                    eng.wait_ge(parts_ready, a + 1)
                for h, cols in halves():
                    last = nc.tensor.matmul(att[:, use.unit, cols], spread_sel[:, 3 * i + n, :], parts[:, g, cols],
                                            start=True, stop=True)
                last.then_inc(att_full, 1)

            def attention_map(p, g, i):
                use = Use(p, ("map", i))
                claim(use)
                for h, cols in halves():
                    last = nc.tensor.matmul(att[:, use.unit, cols], spread_sel[:, 3 * i + 2, :], parts[:, g, cols],
                                            start=True, stop=True)
                last.then_inc(att_full, 1)

            def logits(p, a):
                use = Use(p, ("logits",))
                claim(use)
                eng.wait_ge(gated_ready, a + 1)
                nc.tensor.matmul(att[:, use.unit, 0:GP * K], same_image[:, :],
                                 zt[:, 0, :, :], start=True, stop=True).then_inc(att_full, 1)

            def beside(p, j, at, a, g, final):
                for key, behind in slot_uses(j, final):
                    if behind == at:
                        if key[0] == "map":
                            attention_map(p, a[1] if key[1] == 0 else g, key[1])
                        elif key[0] == "gn":
                            group_average(p, 4, 0, GP, NP + RESIDUAL.index(GP - 1) + 1)
                        elif key[0] == "scores":
                            scores(p, a[0], a[1])
                        elif key[0] == "spread":
                            spread(p, a[0], a[1], key[1], key[2])
                        elif key[0] == "logits":
                            logits(p, a[0])

            def convolve(p, j, a, g, final=False):
                q = p * GP + j
                s = j % 2
                beside(p, j, -1, a, g, final)
                for at in range(2 * TAPS):
                    n, t = divmod(at, TAPS)
                    kh, kw = divmod(t, 3)
                    if t == 0:
                        eng.wait_ge(xlo_ready, 2 * q + 1 + n)
                        eng.wait_ge(wlo_ready, 2 * q + 1 + n)
                        eng.wait_ge(x_ready, NP + 2 * q - 1 + n)
                    for h, cols in halves():
                        last = nc.tensor.matmul(
                            conv[:, n, cols], ws[n][:, s, t, :],
                            xs[n][:, s, kh + 16 * h:kh + 16 * h + 16, kw:kw + W],
                            start=(t == 0), stop=(t == TAPS - 1))
                    if t == TAPS - 1:
                        last.then_inc(conv_full, 1)
                    beside(p, j, at, a, g, final)

            eng.wait_ge(turn_consts_in, 32)
            for key in PROLOGUE_USES:
                if key[0] == "turn":
                    turn(key[1])
                elif key[0] == "gn":
                    group_average(-1, key[1], CH * key[1], CH * key[1] + CH, CH * key[1] + CH)
                elif key[0] == "scores":
                    eng.wait_ge(setup, WQ_STEP)
                    scores(-1, 0, 0)
                    for k in range(GP + GP // 2 - 1, NP):
                        turn(k)
                elif key[0] == "spread":
                    spread(-1, 0, 0, key[1], key[2])
                elif key[0] == "logits":
                    logits(-1, 0)
                else:
                    attention_map(-1, 0, 0)
            eng.wait_ge(second_emptied, GP)
            with eng.Fori(0, PHASES - 1) as p:
                g = eng.snap(p % 2)
                ng = eng.snap((p + 1) % 2)
                for j in range(GP):
                    convolve(p, j, (p + 1, ng), g)
            for j in range(GP):
                convolve(PHASES - 1, j, None, (PHASES - 1) % 2, final=True)

            def project(k, s, m, weights, rows):
                if not (isinstance(m, int) and m == 0):
                    eng.wait_ge(misc_free, m)
                eng.wait_ge(xn_ready, k + 1)
                for h, cols in halves():
                    last = nc.tensor.matmul(att[0:rows, 1, cols], weights, xn[s][:, cols], start=True, stop=True)
                last.then_inc(misc_full, 1)

            def turn_back(k, m):
                eng.wait_ge(misc_free, m)
                eng.wait_ge(fin_ready, k + 1)
                cols = fin.rearrange("c (p t) -> c t p", t=T)
                for t in range(T):
                    last = nc.tensor.transpose(att[:, 1, 128 * t:128 * t + 128], cols[:, t, :], ident[:, :])
                last.then_inc(misc_full, 1)

            def expand(k, s, kk):
                e = k * TAPS + kk
                unit = (s * TAPS + kk) % 2
                if kk == 0:
                    eng.wait_ge(rstk_ready, k + 1)
                if not (isinstance(k, int) and k == 0 and kk < 2):
                    eng.wait_ge(prod_ready, e - 1)
                for h, cols in halves():
                    last = nc.tensor.matmul(conv[:, unit, cols], wse[:, kk, :], rstk[s][0:RR, cols],
                                            start=True, stop=True)
                last.then_inc(exp_full, 1)

            def add_up(k, s, kk):
                if kk == 0 and not (isinstance(k, int) and k == 0):
                    eng.wait_ge(fin_ready, k)
                if kk == DIRECT:
                    eng.wait_ge(prod_ready, k * TAPS + kk + 1)
                    passes = [(sum_sel[:, kk, :].bitcast(F32), prod[prod_slot(s, kk)])]
                else:
                    if kk in LO_DVE:
                        eng.wait_ge(lo_dve_ready, k * len(LO_DVE) + LO_DVE.index(kk) + 1)
                    else:
                        eng.wait_ge(lo_pool_ready, k * len(LO_POOL) + LO_POOL.index(kk) + 1)
                    slot = SPLIT.index(kk) % RING
                    passes = [(sum_sel[:, kk, :], hi[slot]), (sum_sel[:, kk, :], lo[slot])]
                for n, (sel, src) in enumerate(passes):
                    for h, cols in halves():
                        last = nc.tensor.matmul(att[:, 0, cols], sel, src[:, cols], start=(kk == 0 and n == 0),
                                                stop=(kk == TAPS - 1 and n == len(passes) - 1))
                last.then_inc(sum_done, 1)

            def involve(k, s, first=False, last=False):
                for kk in range(TAPS):
                    expand(k, s, kk)
                    if kk >= LAG:
                        add_up(k, s, kk - LAG)
                    elif not first:
                        add_up(k - 1, 1 - s, TAPS + kk - LAG)
                    m = 2 if first else 3 * k + 2
                    if kk == LAG - 1 and not last:
                        project(k + 1, 1 - s, m, wr[:, :], AR)
                    if kk == LAG + 1 and not last:
                        project(k + 1, 1 - s, m + 1, wi[:, :], 128)
                    if kk == T_AT and not first:
                        turn_back(k - 1, m if last else m + 2)

            project(0, 0, 0, wr[:, :], AR)
            project(0, 0, 1, wi[:, :], 128)
            eng.wait_ge(wse_ready, 1)
            eng.wait_ge(late_setup, LATE_STEPS)
            involve(0, 0, first=True)
            eng.wait_ge(misc_free, 4)
            eng.wait_ge(mv_ready, 2 * NP)
            nc.tensor.matmul(att[:, 1, 0:2 * GP], pair_avg[:, :], mv[:, GP:NP, :], start=True, stop=True)\
                .then_inc(misc_full, 1)
            with eng.Fori(0, GP - 1) as i:
                involve(2 * i + 1, 1)
                involve(2 * i + 2, 0)
            involve(NP - 1, 1, last=True)
            for kk in range(TAPS - LAG, TAPS):
                add_up(NP - 1, 1, kk)
            turn_back(NP - 1, 3 * NP)

        @block.scalar
        def _(eng):
            eng.dma_start(ident[:, :], A["c_ident"]).then_inc(turn_consts_in, 16)
            eng.dma_start(pair_avg[:, :], A["c_pair"]).then_inc(turn_consts_in, 16)

            def softplus():
                eng.wait_ge(setup, 2)
                nc.scalar.activation(sp[:, 1:2], sp[:, 0:1], ACT.Exp, scale=-1.0).then_inc(setup_act, 1)
                eng.wait_ge(setup_act, 1)
                nc.scalar.activation(sp[:, 2:3], sp[:, 1:2], ACT.Ln, bias=one[:, 0:1]).then_inc(setup_act, 1)

            def turned(k):
                if k < GP:
                    use = Use(-1, ("turn", k))
                    eng.wait_ge(att_full, use.full)
                    unit, freed = att[:, use.unit, :], att_free[use.unit]
                else:
                    eng.wait_ge(second_turned, k - GP + 1)
                    unit, freed = conv[:, k % 2, :], second_emptied
                nc.scalar.activation(xin[:, k, :].rearrange("c (p t) -> c p t", t=T),
                                     unit.rearrange("c (t p) -> c p t", t=T), ACT.Copy).then_inc(freed, 1)

            def normalise(c):
                eng.wait_ge(nmr_ready, c + 1)
                for k in range(c * CH, (c + 1) * CH):
                    nc.scalar.activation(x[:, k, :], xin[:, k, :], ACT.Identity, bias=nmr[:, k:k + 1],
                                         scale=rstd[:, k:k + 1]).then_inc(x_ready, 1)

            def exponentials(p, a):
                use = Use(p, ("scores",))
                eng.wait_ge(negmax_ready, a + 1)
                nc.scalar.activation(attn, att[0:AR, use.unit, :], ACT.Exp, bias=soft[:, 1:2],
                                     accum_out=soft[:, 2:3]).then_inc(att_free[use.unit], 1)

            def route_exp(a):
                eng.wait_ge(shifted_ready, a + 1)
                nc.scalar.activation(rt[:, 3, :, :], rt[:, 2, :, :], ACT.Exp, scale=1.0 / TEMP).then_inc(rexp_ready, 1)

            def factor(p, use, q):
                eng.wait_ge(att_full, use.full)
                if not (isinstance(q, int) and q == 0):
                    eng.wait_ge(xlo_ready, 2 * q)
                nc.scalar.activation(xm[:, :], att[:, use.unit, :], ACT.Identity, bias=one[:, 0:1],
                                     scale=gain[:, 0:1]).then_inc(att_free[use.unit], 1)

            def begin_combine(i, q):
                if not (isinstance(q, int) and q == 0):
                    eng.wait_ge(wlo_ready, 2 * q)
                nc.scalar.activation(comb[:, :, :].rearrange("p a b -> p (a b)"), experts[:, 0, :], ACT.Identity,
                                     scale=wsel[:, i, 0:1]).then_inc(comb_step, 1)

            def weights_hi(q, s, n):
                if n == 0:
                    eng.wait_ge(comb_step, K * (q + 1))
                for p in (other[n], own[n]):
                    nc.scalar.activation(ws[n][p, s, :, own[n]], comb[own[n], :, :], ACT.Copy).then_inc(whi_ready, 1)

            def x_hi(q, s, n):
                if n == 0:
                    eng.wait_ge(xm_ready, q + 1)
                nc.scalar.activation(inner(xs[n], own[n], s), img(xm[own[n], :]), ACT.Copy).then_inc(xhi_ready, 1)

            def empty_conv(q, n, row, a):
                eng.wait_ge(conv_full, 2 * q + n + 1)
                if n == 0:
                    eng.wait_ge(bias_ready, a + 1)
                nc.scalar.activation(main[other[n], :], conv[own[n], n, :], ACT.Identity,
                                     bias=bias[own[n], bass.ds(row, 1)]).then_inc(main_ready, 1)

            def expanded_weights():
                late = Steps(eng, late_setup)
                eng.wait_ge(late_consts_in, 16 * len(LATE_CONSTS))
                late.then(nc.scalar.activation(
                    st_exp.rearrange("p (g j t) -> p g j t", g=G16, j=C // G16),
                    st_ws.rearrange("p (g t) -> p g t", g=G16).unsqueeze(2).to_broadcast([RR, G16, C // G16, TAPS]), ACT.Copy))
                for n in range(2):
                    late.then(nc.scalar.activation(st_bd[:, :, 64 * n:64 * n + 64], st_exp.rearrange("p (t c) -> p t c", t=TAPS),
                                                   ACT.Identity, scale=masks[:, n:n + 1]))
                late.then(nc.scalar.activation(wse[:, :, :], st_bd, ACT.Copy))
                late.then(nc.scalar.activation(sum_sel[:, :, :].rearrange("p a b -> p (a b)"), st_sum, ACT.Copy))
                assert late.n == LATE_STEPS

            def phase(p, g, attend):
                for j in range(GP):
                    q = p * GP + j
                    s = (j + 1) % 2
                    row = g * GP + j
                    if j == 0:
                        begin_combine(1, q + 1)
                        factor(p, Use(p, ("map", 1)), q + 1)
                        weights_hi(q + 1, s, 0)
                        weights_hi(q + 1, s, 1)
                        x_hi(q + 1, s, 0)
                        if attend:
                            exponentials(p, p + 1)
                        x_hi(q + 1, s, 1)
                        empty_conv(q, 0, row, p)
                        begin_combine(2, q + 2)
                        empty_conv(q, 1, row, p)
                    elif j < GP - 1:
                        factor(p, Use(p, ("map", j + 1)), q + 1)
                        weights_hi(q + 1, s, 0)
                        weights_hi(q + 1, s, 1)
                        x_hi(q + 1, s, 0)
                        empty_conv(q, 0, row, p)
                        x_hi(q + 1, s, 1)
                        if j < GP - 2:
                            begin_combine(j + 2, q + 2)
                        empty_conv(q, 1, row, p)
                    elif attend:
                        factor(p, Use(p, ("map", 0)), q + 1)
                        x_hi(q + 1, s, 0)
                        route_exp(p + 1)
                        empty_conv(q, 0, row, p)
                        x_hi(q + 1, s, 1)
                        empty_conv(q, 1, row, p)
                        eng.wait_ge(route_step, ROUTE_STEPS * (p + 1) + WSEL_STEP)
                        begin_combine(0, q + 1)
                        weights_hi(q + 1, s, 0)
                        weights_hi(q + 1, s, 1)
                    else:
                        expanded_weights()
                        empty_conv(q, 0, row, p)
                        empty_conv(q, 1, row, p)

            for k in range(GP):
                turned(k)
            normalise(0)
            normalise(1)
            softplus()
            for k in range(GP, GP + CH - 1):
                turned(k)
            exponentials(-1, 0)
            for k in range(GP + CH - 1, NP):
                turned(k)
            normalise(2)
            normalise(3)
            route_exp(0)
            eng.wait_ge(setup_done, 1)
            eng.wait_ge(pads_in, 4)
            factor(-1, Use(-1, ("map", 0)), 0)
            eng.wait_ge(route_step, WSEL_STEP)
            begin_combine(0, 0)
            for n in range(2):
                weights_hi(0, 0, n)
                x_hi(0, 0, n)
            with eng.Fori(0, PHASES - 1) as p:
                g = eng.snap(p % 2)
                phase(p, g, True)
            phase(PHASES - 1, (PHASES - 1) % 2, False)

            eng.wait_ge(nmr_ready, 5)
            eng.wait_ge(pads_zeroed, 4)

            def normalise2(k, s):
                nc.scalar.activation(xn[s], xin[:, k, :], ACT.Identity, bias=nmr[:, bass.ds(k, 1)],
                                     scale=rstd[:, bass.ds(k, 1)]).then_inc(xn_ready, 1)

            def empty_xi(s, m):
                eng.wait_ge(misc_full, m + 1)
                nc.scalar.activation(xip[s][:, 1:H + 1, 1:W + 1], img(att[:, 1, :]), ACT.Identity, bias=bi_s[:, 0:1])\
                    .then_inc(misc_free, 1)

            def empty_r(k, s, m):
                eng.wait_ge(misc_full, m + 1)
                if not (isinstance(k, int) and k == 0):
                    eng.wait_ge(rstk_ready, k)
                nc.scalar.activation(r96, att[0:AR, 1, :], ACT.Relu, bias=rsc[:, 3:4], scale=rsc[:, 1:2])\
                    .then_inc(misc_free, 1)
                eng.wait_ge(misc_free, m + 1)
                nc.scalar.activation(rstk[s][0:AR, :], r96, ACT.Copy).then_inc(rhi_ready, 1)

            def split_prod(k, s, kk, first):
                n = SPLIT.index(kk)
                eng.wait_ge(prod_ready, k * TAPS + kk + 1)
                if not (first and n < RING):
                    eng.wait_ge(sum_done, (k if n >= RING else k - 1) * TAPS + SPLIT[n - RING] + 1)
                nc.scalar.activation(hi[n % RING], prod[prod_slot(s, kk)], ACT.Copy).then_inc(hi_ready, 1)

            def empty_pix(k, s, m):
                eng.wait_ge(misc_full, m + 1)
                if not (isinstance(k, int) and k < 2):
                    eng.wait_ge(stored[s], (k - s) * 16)
                nc.scalar.activation(pix[s], att[:, 1, :].rearrange("p (t c) -> p t c", t=T), ACT.Copy)\
                    .then_inc(misc_free, 1)

            def involve(k, s, first=False, last=False):
                m = 2 if first else 3 * k + 2
                if not last:
                    normalise2(k + 1, 1 - s)
                for kk in range(TAPS):
                    if kk != DIRECT:
                        split_prod(k, s, kk, first)
                    if kk == 4 and not last:
                        empty_r(k + 1, 1 - s, m)
                    if kk == 6 and not last:
                        empty_xi(1 - s, m + 1)
                    if kk == 8 and not first:
                        empty_pix(k - 1, 1 - s, m if last else m + 2)

            normalise2(0, 0)
            empty_r(0, 0, 0)
            empty_xi(0, 1)
            involve(0, 0, first=True)
            involve(1, 1)
            involve(2, 0)
            eng.wait_ge(nmr_ready, 6)
            with eng.Fori(1, GP - 1) as i:
                involve(2 * i + 1, 1)
                involve(2 * i + 2, 0)
            involve(NP - 1, 1, last=True)
            empty_pix(NP - 1, 1, 3 * NP)

        @block.vector
        def _(eng):
            v = nc.vector
            st = Steps(eng, setup)

            for t in (wi, wr, wq8):
                v.memset(t[:, :], 0.0).then_inc(zeroed, 1)
            eng.wait_ge(zeroed, ZEROS)
            gn = Steps(eng, gn_step)

            def group_norm(src, lo_k, hi_k, full, freed):
                n = hi_k - lo_k
                avg = src.rearrange("p (k s) -> p k s", s=2)
                rows = mv[:, lo_k:hi_k, :]
                eng.wait_ge(full[0], full[1])
                gn.then(v.tensor_scalar(negmean[:, lo_k:hi_k], avg[:, :, 0], -1.0, None, ALU.mult))
                v.tensor_scalar(gnt[:, 1, 0:n], avg[:, :, 1], GN_EPS, None, ALU.add).then_inc(freed[0], 1)
                eng.wait_ge(freed[0], freed[1])
                gn.then(v.tensor_tensor(gnt[:, 2, 0:n], rows[:, :, 0], negmean[:, lo_k:hi_k], ALU.add))
                gn.then(v.tensor_tensor(gnt[:, 3, 0:n], gnt[:, 2, 0:n], gnt[:, 2, 0:n], ALU.mult))
                v.tensor_tensor(variance[:, lo_k:hi_k], gnt[:, 3, 0:n], gnt[:, 1, 0:n], ALU.add)\
                    .then_inc(variance_ready, 1)

            so = Steps(eng, soft_step)

            def row_max(p, a):
                use = Use(p, ("scores",))
                so.start(SOFT_STEPS * a)
                eng.wait_ge(att_full, use.full)
                so.then(v.tensor_reduce(soft[:, 0:1], att[0:AR, use.unit, :], AX.X, ALU.max))
                v.tensor_scalar(soft[:, 1:2], soft[:, 0:1], -1.0, None, ALU.mult).then_inc(negmax_ready, 1)

            def softmax(p, a, g):
                use = Use(p, ("scores",))
                eng.wait_ge(att_free[use.unit], use.freed)
                so.then(v.reciprocal(soft[:, 3:4], soft[:, 2:3]))
                so.then(v.tensor_scalar(attn, attn, soft[:, 3:4], None, ALU.mult))
                so.then(v.tensor_copy(parts[:, g, :], attn))
                so.then(v.tensor_tensor(attn, attn, parts[:, g, :], ALU.subtract))
                so.then(v.tensor_copy(parts[32:64, g, :], attn[32:64, :]))
                so.then(v.tensor_copy(parts[64:AR, g, :], attn[64:AR, :]))
                assert so.n == SOFT_STEPS
                v.tensor_tensor(parts[64:AR, g, :], attn[64:AR, :], parts[64:AR, g, :], ALU.subtract)\
                    .then_inc(parts_ready, 1)

            def pool(p, a, g, i, n):
                use = Use(p, ("spread", i, n))
                if i == 0 and n == 0:
                    eng.wait_ge(parts_ready, a + 1)
                else:
                    before = Use(p, ("spread", i - 1 + n, 1 - n))
                    eng.wait_ge(att_free[before.unit], before.freed)
                eng.wait_ge(att_full, use.full)
                v.scalar_tensor_tensor(work[:, :], att[:, use.unit, :], 1.0, x[:, g * GP + i, :], ALU.mult, ALU.mult,
                                       accum_out=pooled[:, i, n:n + 1]).then_inc(att_free[use.unit], 1)

            def bc(ap, axis, shape):
                return ap.unsqueeze(axis).to_broadcast(shape)

            r = Steps(eng, route_step)
            sh = [128, GP, K]

            def gated(p, a):
                r.start(ROUTE_STEPS * a)
                for n in range(HEADS):
                    use = Use(p, ("spread", GP - 1, n))
                    eng.wait_ge(att_free[use.unit], use.freed)
                for n in range(HEADS):
                    r.then(v.tensor_tensor(zt[:, n, :, :], bc(pooled[:, :, n], 2, sh), bc(gate[:, n, :], 1, sh), ALU.mult))
                v.tensor_tensor(zt[:, 0, :, :], zt[:, 0, :, :], zt[:, 1, :, :], ALU.add).then_inc(gated_ready, 1)

            def route(p, a, g):
                use = Use(p, ("logits",))
                eng.wait_ge(att_full, use.full)
                ok = allowed[:, g, :, :]
                v.tensor_tensor(rt[:, 0, :, :], att[:, use.unit, 0:GP * K].rearrange("p (i k) -> p i k", k=K), ok,
                                ALU.mult).then_inc(att_free[use.unit], 1)
                eng.wait_ge(att_free[use.unit], use.freed)
                r.then(v.tensor_scalar(rt[:, 1, :, :], ok, -1.0, 1e9, ALU.add, ALU.mult))
                r.then(v.tensor_tensor(rt[:, 0, :, :], rt[:, 0, :, :], rt[:, 1, :, :], ALU.add))
                r.then(v.tensor_reduce(rs[:, 0, :], rt[:, 0, :, :], AX.X, ALU.max))
                v.tensor_tensor(rt[:, 2, :, :], rt[:, 0, :, :], bc(rs[:, 0, :], 2, sh), ALU.subtract)\
                    .then_inc(shifted_ready, 1)
                eng.wait_ge(rexp_ready, a + 1)
                r.then(v.tensor_reduce(rs[:, 1, :], rt[:, 3, :, :], AX.X, ALU.add))
                r.then(v.reciprocal(rs[:, 2, :], rs[:, 1, :]))
                w = rt[:, 4, :, :]
                r.then(v.tensor_tensor(w, rt[:, 3, :, :], bc(rs[:, 2, :], 2, sh), ALU.mult))
                full = [128, GP, K, K]
                wj, we = bc(w, 2, full), bc(w, 3, full)
                r.then(v.tensor_tensor(cmp[:, 0, :, :, :], wj, we, ALU.is_gt))
                r.then(v.tensor_tensor(cmp[:, 1, :, :, :], wj, we, ALU.is_equal))
                r.then(v.tensor_tensor(cmp[:, 2, :, :, :], cmp[:, 1, :, :, :], bc(earlier[:, :, :], 1, full), ALU.mult))
                r.then(v.tensor_tensor(cmp[:, 1, :, :, :], cmp[:, 2, :, :, :], cmp[:, 0, :, :, :], ALU.add))
                r.then(v.tensor_reduce(rt[:, 5, :, :], cmp[:, 1, :, :, :], AX.X, ALU.add))
                r.then(v.tensor_scalar(rt[:, 6, :, :], rt[:, 5, :, :], 1.5, None, ALU.is_lt))
                r.then(v.tensor_tensor(rt[:, 7, :, :], w, rt[:, 6, :, :], ALU.mult))
                r.then(v.tensor_reduce(rs[:, 3, :], rt[:, 7, :, :], AX.X, ALU.add))
                r.then(v.tensor_scalar(rs[:, 4, :], rs[:, 3, :], 1e-9, None, ALU.add))
                r.then(v.reciprocal(rs[:, 5, :], rs[:, 4, :]))
                r.then(v.tensor_tensor(wsel[:, :, :], rt[:, 7, :, :], bc(rs[:, 5, :], 2, sh), ALU.mult))
                assert r.n == WSEL_STEP

            def next_mask_and_bias(g):
                r.then(v.tensor_scalar(rt[:, 8, :, :], rt[:, 5, :, :], 0.5, None, ALU.is_lt))
                some = allowed[:, g, :, 0:K - 1]
                r.then(v.tensor_tensor(rt[:, 9, :, 0:K - 1], some, rt[:, 8, :, 0:K - 1], ALU.subtract))
                r.then(v.tensor_scalar(some, rt[:, 9, :, 0:K - 1], 0.0, 1.0, ALU.max, ALU.min))
                r.then(v.tensor_tensor(rt[:, 10, :, :], wsel[:, :, :], bc(be_s[:, :], 1, sh), ALU.mult))
                assert r.n == ROUTE_STEPS
                v.tensor_reduce(bias[:, bass.ds(g * GP, GP)] if not isinstance(g, int) else bias[:, g * GP:(g + 1) * GP],
                                rt[:, 10, :, :], AX.X, ALU.add).then_inc(bias_ready, 1)

            def modulate(p, g, i, q):
                use = Use(p, ("map", i))
                eng.wait_ge(att_free[use.unit], use.freed)
                v.tensor_tensor(xm[:, :], xm[:, :], x[:, g * GP + i, :], ALU.mult).then_inc(xm_ready, 1)

            def combine(i, q):
                cflat = comb[:, :, :].rearrange("p a b -> p (a b)")
                for e in range(1, K):
                    eng.wait_ge(comb_step, K * q + e)
                    v.scalar_tensor_tensor(cflat, experts[:, e, :], wsel[:, i, e:e + 1], cflat, ALU.mult, ALU.add)\
                        .then_inc(comb_step, 1)

            def add_lo(q, n, row):
                eng.wait_ge(main_ready, 2 * q + n + 1)
                v.tensor_tensor(x[own[n], row, :], main[other[n], :], conv[other[n], n, :], ALU.add)\
                    .then_inc(x_ready, 1)

            def channel_stats(k):
                for n in range(2):
                    gn.then(v.bn_stats(stats[:, k, n, :], xin[:, k, n * HW:(n + 1) * HW]))
                v.bn_aggr(mv[:, k, :], stats[:, k, :, :]).then_inc(mv_ready, 1)

            def turned_stats(k):
                if k < GP:
                    use = Use(-1, ("turn", k))
                    eng.wait_ge(att_free[use.unit], use.freed)
                else:
                    eng.wait_ge(second_emptied, k - GP + 1)
                channel_stats(k)

            def chunk_norm(c):
                use = Use(-1, ("gn", c))
                group_norm(att[:, use.unit, 0:2 * CH], CH * c, CH * c + CH, (att_full, use.full),
                           (att_free[use.unit], use.freed))

            def residual(n):
                k = RESIDUAL[n]
                eng.wait_ge(x_ready, NP + 2 * GP * (PHASES - 1) + (2 * (k - GP + 1) if k >= GP else 0))
                v.tensor_tensor(xin[:, k, :], xin[:, k, :], x[:, k, :], ALU.add).then_inc(x1_step, 1)
                eng.wait_ge(x1_step, n + 1)
                channel_stats(k)

            def constants_ready():
                st.start(0)
                eng.wait_ge(consts_in, CONSTS_IN)
                st.then(v.memset(one[:, :], 1.0))
                st.then(v.scalar_tensor_tensor(sp[:, 0:1], alpha[:, :], -1.0, alpha[:, :], ALU.mult, ALU.max))
                st.then(v.tensor_scalar(rsc[:, 0:1], rpar[:, 4:5], BN_EPS, None, ALU.add))
                assert st.n == POW_STEP
                st.then(v.tensor_tensor(tmp32[:, 0:2, 0, :], wk_s[:, :].rearrange("p (n d) -> p n d", n=HEADS),
                                        q_s[:, :].rearrange("p (n d) -> p n d", n=HEADS), ALU.mult))
                st.then(v.tensor_reduce(wq[:, :], tmp32[:, 0:2, 0, :], AX.X, ALU.add))
                for part in range(PARTS):
                    for n in range(2):
                        p = slice(64 * n, 64 * n + 64)
                        dst = wq8[p, :].rearrange("p (i r) -> p i r", r=AR + 4)[:, :, 32 * part + 2 * n:32 * part + 2 * n + 2]
                        st.then(v.tensor_scalar(dst, wq[p, :].unsqueeze(1).to_broadcast([64, GP, HEADS]),
                                                DH ** -0.5, None, ALU.mult))
                assert st.n == WQ_STEP

            def late_constants_ready():
                st.then(v.tensor_tensor(
                    tmp32[:, :, :, :],
                    wv_s[:, :].rearrange("p (n d) -> p n d", n=HEADS).unsqueeze(2).to_broadcast([128, HEADS, K, DH]),
                    wm_s[:, :].rearrange("p (n d k) -> p n k d", n=HEADS, d=DH), ALU.mult))
                st.then(v.tensor_reduce(gate[:, :, :], tmp32[:, :, :, :], AX.X, ALU.add))
                eng.wait_ge(setup_pool, 2)
                st.then(v.tensor_tensor(rsc[:, 1:2], rsc[:, 2:3], rpar[:, 1:2], ALU.mult))
                st.then(v.tensor_tensor(rsc[:, 2:3], rpar[:, 0:1], rpar[:, 3:4], ALU.subtract))
                st.then(v.scalar_tensor_tensor(rsc[:, 3:4], rsc[:, 2:3], rsc[:, 1:2], rpar[:, 2:3], ALU.mult, ALU.add))
                eng.wait_ge(setup_act, 2)
                st.then(v.tensor_scalar(sp[:, 3:4], alpha[:, :], 0.0, sp[:, 2:3], ALU.max, ALU.add))
                st.then(v.tensor_scalar(gain[:, :], sp[:, 3:4], float(S) / HEADS, None, ALU.mult))
                v.memset(allowed[:, :, :, :], 1.0).then_inc(setup_done, 1)

            gn.start(0)
            for k in range(CH):
                turned_stats(k)
            chunk_norm(0)
            for k in range(CH, GP):
                turned_stats(k)
            chunk_norm(1)
            constants_ready()
            for k in range(GP, GP + CH - 1):
                turned_stats(k)
            late_constants_ready()
            row_max(-1, 0)
            softmax(-1, 0, 0)
            turned_stats(GP + CH - 1)
            chunk_norm(2)
            for i in range(GP):
                for n in range(HEADS):
                    pool(-1, 0, 0, i, n)
                if i < CH:
                    turned_stats(GP + CH + i)
                if i == CH + 1:
                    chunk_norm(3)
            gated(-1, 0)
            route(-1, 0, 0)
            combine(0, 0)
            next_mask_and_bias(0)
            modulate(-1, 0, 0, 0)


            def phase(p, g, ng, attend):
                for j in range(GP):
                    q = p * GP + j
                    row = g * GP + j
                    pools = [key for key, _ in slot_uses(j) if attend and key[0] == "spread"]
                    if j == 0:
                        combine(1, q + 1)
                    if j == GP - 1 and attend:
                        gated(p, p + 1)
                        modulate(p, ng, 0, q + 1)
                        route(p, p + 1, ng)
                        combine(0, q + 1)
                        next_mask_and_bias(ng)
                    elif j < GP - 1:
                        modulate(p, g, j + 1, q + 1)
                    if j == 0:
                        if attend:
                            row_max(p, p + 1)
                            softmax(p, p + 1, ng)
                        add_lo(q, 0, row)
                        combine(2, q + 2)
                        for key in pools:
                            pool(p, p + 1, ng, key[1], key[2])
                    else:
                        for key in pools[:1]:
                            pool(p, p + 1, ng, key[1], key[2])
                        if not attend:
                            residual(RESIDUAL.index(j))
                        add_lo(q, 0, row)
                        for key in pools[1:2]:
                            pool(p, p + 1, ng, key[1], key[2])
                        if j < GP - 2:
                            combine(j + 2, q + 2)
                        for key in pools[2:]:
                            pool(p, p + 1, ng, key[1], key[2])
                    if not attend and j == 0:
                        residual(0)
                    if not attend and j >= 2:
                        residual(RESIDUAL.index(j) + 1)
                    add_lo(q, 1, row)

            with eng.Fori(0, PHASES - 1) as p:
                g = eng.snap(p % 2)
                ng = eng.snap((p + 1) % 2)
                phase(p, g, ng, True)
            phase(PHASES - 1, (PHASES - 1) % 2, None, False)

            use = Use(PHASES - 1, ("gn", 4))
            group_norm(att[:, use.unit, 0:2 * GP], 0, GP, (att_full, use.full), (att_free[use.unit], use.freed))
            residual(NP - 2)
            residual(NP - 1)
            eng.wait_ge(late_lo, 2)
            hi_of = wse[:, :, :].rearrange("p a b -> p (a b)")
            v.scalar_tensor_tensor(hi_of, hi_of.bitcast(F32), masks[:, 3:4], st_bd.rearrange("p t c -> p (t c)"),
                                   ALU.mult, ALU.add).then_inc(wse_ready, 1)

            def product(k, s, kk, first, second):
                e = k * TAPS + kk
                unit = (s * TAPS + kk) % 2
                kh, kw = divmod(kk, 3)
                eng.wait_ge(exp_full, e + 1)
                if kk == 0:
                    eng.wait_ge(misc_free, 2 if first else 3 * k + 1)
                old = (kk - PRODS) % TAPS
                before = k if kk >= PRODS else k - 1
                if not (first and kk < PRODS):
                    if old == DIRECT:
                        eng.wait_ge(sum_done, before * TAPS + old + 1)
                    elif old in LO_POOL:
                        eng.wait_ge(lo_pool_ready, before * len(LO_POOL) + LO_POOL.index(old) + 1)
                    else:
                        eng.wait_ge(lo_dve_ready, before * len(LO_DVE) + LO_DVE.index(old) + 1)
                v.tensor_tensor(img(prod[prod_slot(s, kk)]), img(conv[:, unit, :]), xip[s][:, kh:kh + H, kw:kw + W], ALU.mult)\
                    .then_inc(prod_ready, 1)

            def split_lo(k, s, kk):
                slot = SPLIT.index(kk) % RING
                eng.wait_ge(hi_ready, k * len(SPLIT) + SPLIT.index(kk) + 1)
                v.tensor_tensor(lo[slot], prod[prod_slot(s, kk)], hi[slot].bitcast(F32), ALU.subtract).then_inc(lo_dve_ready, 1)

            def finish(k, m):
                eng.wait_ge(sum_done, TAPS * (k + 1))
                if m is not None:
                    eng.wait_ge(misc_full, m)
                v.tensor_tensor(fin, att[:, 0, :], xin[:, k, :], ALU.add).then_inc(fin_ready, 1)

            def involve(k, s, first=False, second=False):
                for kk in range(TAPS):
                    product(k, s, kk, first, second)
                    if kk - 2 in LO_DVE:
                        split_lo(k, s, kk - 2)
                    if kk == LAG - 1 and not first:
                        finish(k - 1, None if second else 3 * k + 2)

            involve(0, 0, first=True)
            group_norm(att[:, 1, 0:2 * GP], GP, NP, (misc_full, 5), (misc_free, 5))
            involve(1, 1, second=True)
            involve(2, 0)
            with eng.Fori(1, GP - 1) as i:
                involve(2 * i + 1, 1)
                involve(2 * i + 2, 0)
            involve(NP - 1, 1)
            finish(NP - 1, 3 * NP)

        @block.gpsimd
        def _(eng):
            v = nc.gpsimd
            v.memset(mhalf[:, :], -0.5).then_inc(setup_pool, 1)
            for t in (xa, wa, xb, wb):
                v.memset(t[:, :, :, :].bitcast(F32), 0.0).then_inc(pads_in, 1)
            eng.wait_ge(pads_in, 4)
            eng.wait_ge(setup_pool, 1)

            def inverse_root(c, lo_k, hi_k):
                n = hi_k - lo_k
                eng.wait_ge(variance_ready, c + 1)
                v.tensor_tensor(rstd[:, lo_k:hi_k], variance[:, lo_k:hi_k], mhalf[:, 0:n], ALU.pow)\
                    .then_inc(inverse_ready, 1)
                eng.wait_ge(inverse_ready, c + 1)
                v.tensor_tensor(nmr[:, lo_k:hi_k], negmean[:, lo_k:hi_k], rstd[:, lo_k:hi_k], ALU.mult)\
                    .then_inc(nmr_ready, 1)

            def split_lo(q, s, x_first=False):
                steps = [("x", 0), ("x", 1), ("w", 0), ("w", 1)] if x_first else [("w", 0), ("w", 1), ("x", 0), ("x", 1)]
                for what, n in steps:
                    if what == "w":
                        eng.wait_ge(whi_ready, 4 * q + 2 * n + 2)
                        v.tensor_tensor(ws[n][own[n], s, :, other[n]], comb[own[n], :, :],
                                        ws[n][own[n], s, :, own[n]].bitcast(F32), ALU.subtract).then_inc(wlo_ready, 1)
                        eng.wait_ge(wlo_ready, 2 * q + n + 1)
                    else:
                        eng.wait_ge(xhi_ready, 2 * q + n + 1)
                        v.tensor_tensor(inner(xs[n], other[n], s), img(xm[own[n], :]),
                                        inner(xs[n], own[n], s).bitcast(F32), ALU.subtract).then_inc(xlo_ready, 1)
                        eng.wait_ge(xlo_ready, 2 * q + n + 1)

            for c in range(2):
                inverse_root(c, CH * c, CH * c + CH)
            eng.wait_ge(setup, POW_STEP)
            eng.wait_ge(nmr_ready, 2)
            v.tensor_tensor(rsc[:, 2:3], rsc[:, 0:1], mhalf[0:AR, 0:1], ALU.pow).then_inc(setup_pool, 1)
            eng.wait_ge(setup_pool, 2)
            inverse_root(2, 2 * CH, 3 * CH)
            inverse_root(3, 3 * CH, NP)
            eng.wait_ge(nmr_ready, 4)
            split_lo(0, 0)
            with eng.Fori(0, PHASES - 1) as p:
                for j in range(GP):
                    split_lo(p * GP + j + 1, (j + 1) % 2, x_first=(j == GP - 1))
            for j in range(GP - 1):
                split_lo((PHASES - 1) * GP + j + 1, (j + 1) % 2)

            eng.wait_ge(xlo_ready, 2 * PHASES * GP)
            eng.wait_ge(late_setup, LATE_STEPS - 1)
            bd = st_bd.rearrange("p t c -> p (t c)")
            v.tensor_tensor(bd, bd, wse[:, :, :].rearrange("p a b -> p (a b)").bitcast(F32), ALU.subtract).then_inc(late_lo, 1)
            eng.wait_ge(late_lo, 1)
            eng.wait_ge(x1_step, RESIDUAL.index(GP + 3) + 1)
            for n in range(2):
                v.memset(xip[n], 0.0).then_inc(pads_zeroed, 1)
                eng.wait_ge(pads_zeroed, 2 * n + 1)
                v.memset(rstk[n][AR:RR, :].bitcast(F32), 1.0).then_inc(pads_zeroed, 1)
                eng.wait_ge(pads_zeroed, 2 * n + 2)
            inverse_root(4, 0, GP)
            v.tensor_scalar(bd, bd, masks[:, 2:3], None, ALU.mult).then_inc(late_lo, 1)

            def r_lo(k, s):
                if isinstance(k, int) and k == 0:
                    eng.wait_ge(nmr_ready, 5)
                else:
                    eng.wait_ge(lo_pool_ready, (k - 1) * len(LO_POOL) + LO_POOL.index(R_AFTER) + 1)
                eng.wait_ge(rhi_ready, k + 1)
                v.tensor_tensor(rstk[s][32:64, :], r96[32:64, :], rstk[s][32:64, :].bitcast(F32), ALU.subtract)\
                    .then_inc(rstk_ready, 1)
                eng.wait_ge(rstk_ready, k + 1)

            def involve(k, s, last=False):
                for kk in range(TAPS):
                    if kk in LO_POOL:
                        slot = SPLIT.index(kk) % RING
                        eng.wait_ge(hi_ready, k * len(SPLIT) + SPLIT.index(kk) + 1)
                        v.tensor_tensor(lo[slot], prod[prod_slot(s, kk)], hi[slot].bitcast(F32), ALU.subtract)\
                            .then_inc(lo_pool_ready, 1)
                    if kk == R_AFTER and not last:
                        r_lo(k + 1, 1 - s)

            eng.wait_ge(late_lo, 2)
            r_lo(0, 0)
            involve(0, 0)
            eng.wait_ge(rstk_ready, 2)
            inverse_root(5, GP, NP)
            involve(1, 1)
            with eng.Fori(1, GP - 1) as i:
                involve(2 * i, 0)
                involve(2 * i + 1, 1)
            involve(NP - 2, 0)
            involve(NP - 1, 1, last=True)


def constants():
    rows = np.arange(AR)
    spread = np.zeros((AR, GP, 3, 128), np.float32)
    for i in range(GP):
        for image in range(2):
            for head in range(HEADS):
                hit = rows % 32 == 4 * i + 2 * image + head
                spread[hit, i, head, 64 * image:64 * image + 64] = 1
                spread[hit, i, 2, 64 * image:64 * image + 64] = 1
    ch = np.arange(128)
    total = np.zeros((128, TAPS, 128), np.float32)
    for t in range(TAPS):
        for c in range(C):
            for image in range(2):
                total[64 * image + c, t, 64 * image + (t * C + c) // TAPS] = 1
    row = np.arange(RR)
    low = ((row >= 64) & (row < 96)) | (row == 97)
    masks = np.stack([(row % 32 < CR) | (row >= AR), (row % 32 >= CR) | (row >= AR), low, ~low], 1).astype(np.float32)
    return {
        "c_spread": spread.reshape(AR, -1).astype(np.uint16) * np.uint16(BF16_ONE),
        "c_ident": np.eye(128, dtype=np.float32),
        "c_pair": np.where(ch[:, None] // 2 == ch // 2, 0.5, 0).astype(np.float32),
        "c_same": (ch[:, None] // 64 == ch // 64).astype(np.float32),
        "c_sum": total.reshape(128, -1),
        "c_masks": masks,
        "c_earlier": np.tril(np.ones((K, K), np.float32), -1).reshape(1, -1)[0],
    }


def kernel(**inputs):
    import concourse.bacc as bacc
    from concourse.bass_utils import run_bass_kernel_spmd

    a = {n: np.ascontiguousarray(v) for n, v in inputs.items()}
    arrays = {
        "x": a["x"].reshape(B, S, C),
        "q": a["L0_conv_q"].reshape(D), "Wk": a["L0_conv_Wk"], "Wv": a["L0_conv_Wv"],
        "Wmlp": a["L0_conv_Wmlp"].reshape(D * K), "alpha": a["L0_conv_alpha"].reshape(1),
        "We": a["L0_conv_We"].reshape(K * TAPS, C, C), "be": np.ascontiguousarray(a["L0_conv_be"].T),
        "rpar": np.ascontiguousarray(np.tile(np.stack(
            [a["L1_conv_" + n] for n in ("br", "gamma", "beta", "mean", "var")], 1), (2 * PARTS, 1))),
        "Wr": a["L1_conv_Wr"], "Ws": a["L1_conv_Ws"], "bs": a["L1_conv_bs"], "Wi": a["L1_conv_Wi"],
        "bi": a["L1_conv_bi"].reshape(C, 1),
        **constants(),
    }
    nc = bacc.Bacc("TRN2", target_bir_lowering=False, num_devices=1)
    A = {n: nc.dram_tensor("in_" + n, v.shape, mybir.dt.from_np(v.dtype), kind="ExternalInput").ap()
         for n, v in arrays.items()}
    out = nc.dram_tensor("out", (B, S, C), F32, kind="ExternalOutput").ap()
    build(nc, A, out)
    r = run_bass_kernel_spmd(nc, [{"in_" + n: v for n, v in arrays.items()}], core_ids=[0])
    return r.results[0]["out"].reshape(B, H, W, C)
```
